# Optimizing a Trainium2 kernel written in Bass

```python
import numpy as np
import jax
import jax.numpy as jnp

def _softmax(x, axis=-1):
    return jax.nn.softmax(x, axis=axis)

def _gelu(x):
    return jax.nn.gelu(x, approximate=True)

def _silu(x):
    return jax.nn.silu(x)

def _sigmoid(x):
    return jax.nn.sigmoid(x)

def _layernorm(x, axis=-1, eps=1e-05):
    m = jnp.mean(x, axis=axis, keepdims=True)
    v = jnp.var(x, axis=axis, keepdims=True)
    return (x - m) / jnp.sqrt(v + eps)

def _scatter_add(tgt, idx, src, axis=0):
    return tgt.at[idx].add(src)

def _segment_sum(src, seg, n):
    return jax.ops.segment_sum(src, seg, n)
kernel_name = 'mk_sandwich_d1_jaxref_r2_2a031b'

def setup_inputs(seed: int=0):
    np.random.seed(seed)
    _w = jnp.asarray

    def _L0_attn_setup():
        import jax, jax.numpy as jnp
        import numpy as np
        NEG = 10000.0
        key = jax.random.key(seed)
        ks = jax.random.split(key, 5)
        B, S, D = (2, 1024, 512)
        std = 1.0 / np.sqrt(D)
        return {'x': jax.random.normal(ks[0], (B, S, D), dtype=jnp.float32), 'Wq': jax.random.normal(ks[1], (D, D), dtype=jnp.float32) * std, 'bq': jnp.zeros((D,), jnp.float32), 'Wk': jax.random.normal(ks[2], (D, D), dtype=jnp.float32) * std, 'bk': jnp.zeros((D,), jnp.float32), 'Wv': jax.random.normal(ks[3], (D, D), dtype=jnp.float32) * std, 'bv': jnp.zeros((D,), jnp.float32), 'Wo': jax.random.normal(ks[4], (D, D), dtype=jnp.float32) * std, 'bo': jnp.zeros((D,), jnp.float32)}
    _L0_attn_in = _L0_attn_setup()

    def _L0_ffn_setup():
        import jax, jax.numpy as jnp
        import numpy as np
        B, L, C1, C2, K, K_IN = (4, 512, 512, 512, 32, 32)
        BN_EPS = 1e-05

        def _gated_bottleneck(x2d, conv_w, conv_b, gamma, beta, lin_w, lin_b):
            n = x2d.shape[0]
            g = conv_w.shape[0]
            xc = jnp.einsum('ngf,gf->ng', x2d.reshape(n, g, 4), conv_w) + conv_b
            mean = jnp.mean(xc, axis=0)
            var = jnp.mean((xc - mean) ** 2, axis=0)
            xn = (xc - mean) * jax.lax.rsqrt(var + BN_EPS) * gamma + beta
            xa = jax.nn.gelu(xn, approximate=False)
            return xa @ lin_w.T + lin_b
        key = jax.random.key(seed)
        ks = jax.random.split(key, 8)
        g = C1 // 4
        w_std = (2.0 / C2) ** 0.5
        lin_std = (1.0 / g) ** 0.5
        return {'x': jax.random.normal(ks[0], (B, L, C1), jnp.float32), 'weight': jax.random.normal(ks[1], (C1, C2), jnp.float32) * w_std, 'bias': jnp.zeros((C2,), jnp.float32), 'so_conv_w': jax.random.normal(ks[2], (g, 4), jnp.float32) * 0.5, 'so_conv_b': jnp.zeros((g,), jnp.float32), 'so_gamma': jnp.ones((g,), jnp.float32), 'so_beta': jnp.zeros((g,), jnp.float32), 'so_lin_w': jax.random.normal(ks[3], (C2, g), jnp.float32) * lin_std, 'so_lin_b': jnp.zeros((C2,), jnp.float32), 'si_conv_w': jax.random.normal(ks[4], (g, 4), jnp.float32) * 0.5, 'si_conv_b': jnp.zeros((g,), jnp.float32), 'si_gamma': jnp.ones((g,), jnp.float32), 'si_beta': jnp.zeros((g,), jnp.float32), 'si_lin_w': jax.random.normal(ks[5], (C1, g), jnp.float32) * lin_std, 'si_lin_b': jnp.zeros((C1,), jnp.float32)}
    _L0_ffn_in = _L0_ffn_setup()
    _d = {'L0_attn_x': _L0_attn_in['x'], 'L0_attn_Wq': _L0_attn_in['Wq'], 'L0_attn_bq': _L0_attn_in['bq'], 'L0_attn_Wk': _L0_attn_in['Wk'], 'L0_attn_bk': _L0_attn_in['bk'], 'L0_attn_Wv': _L0_attn_in['Wv'], 'L0_attn_bv': _L0_attn_in['bv'], 'L0_attn_Wo': _L0_attn_in['Wo'], 'L0_attn_bo': _L0_attn_in['bo'], 'L0_ffn_weight': _L0_ffn_in['weight'], 'L0_ffn_bias': _L0_ffn_in['bias'], 'L0_ffn_so_conv_w': _L0_ffn_in['so_conv_w'], 'L0_ffn_so_conv_b': _L0_ffn_in['so_conv_b'], 'L0_ffn_so_gamma': _L0_ffn_in['so_gamma'], 'L0_ffn_so_beta': _L0_ffn_in['so_beta'], 'L0_ffn_so_lin_w': _L0_ffn_in['so_lin_w'], 'L0_ffn_so_lin_b': _L0_ffn_in['so_lin_b'], 'L0_ffn_si_conv_w': _L0_ffn_in['si_conv_w'], 'L0_ffn_si_conv_b': _L0_ffn_in['si_conv_b'], 'L0_ffn_si_gamma': _L0_ffn_in['si_gamma'], 'L0_ffn_si_beta': _L0_ffn_in['si_beta'], 'L0_ffn_si_lin_w': _L0_ffn_in['si_lin_w'], 'L0_ffn_si_lin_b': _L0_ffn_in['si_lin_b']}
    _x0 = _d['L0_attn_x']
    _d['L0_attn_x'] = jax.random.normal(jax.random.fold_in(jax.random.key(seed), 1), (4, 2048, 512), dtype=_x0.dtype)
    del _x0
    return _d

def reference(L0_attn_x, L0_attn_Wq, L0_attn_bq, L0_attn_Wk, L0_attn_bk, L0_attn_Wv, L0_attn_bv, L0_attn_Wo, L0_attn_bo, L0_ffn_weight, L0_ffn_bias, L0_ffn_so_conv_w, L0_ffn_so_conv_b, L0_ffn_so_gamma, L0_ffn_so_beta, L0_ffn_so_lin_w, L0_ffn_so_lin_b, L0_ffn_si_conv_w, L0_ffn_si_conv_b, L0_ffn_si_gamma, L0_ffn_si_beta, L0_ffn_si_lin_w, L0_ffn_si_lin_b):

    def _L0_attn_ref(x, Wq, bq, Wk, bk, Wv, bv, Wo, bo):
        import jax, jax.numpy as jnp
        import numpy as np
        NEG = 10000.0
        q = jax.nn.relu(x @ Wq + bq)
        k = jax.nn.relu(x @ Wk + bk)
        v = jax.nn.relu(x @ Wv + bv)
        D = q.shape[-1]
        e = jnp.einsum('bqd,bkd->bqk', q, k) / jnp.sqrt(jnp.float32(D))
        S = e.shape[-1]
        causal = (jnp.arange(S)[None, :] > jnp.arange(S)[:, None]).astype(e.dtype)
        e = e - NEG * causal[None, :, :]
        e = jnp.exp(e - jnp.max(e, axis=-1, keepdims=True))
        attn = e / jnp.sum(e, axis=-1, keepdims=True)
        y = jnp.einsum('bqk,bkd->bqd', attn, v)
        return jax.nn.relu(y @ Wo + bo)

    def _L0_ffn_ref(x, weight, bias, so_conv_w, so_conv_b, so_gamma, so_beta, so_lin_w, so_lin_b, si_conv_w, si_conv_b, si_gamma, si_beta, si_lin_w, si_lin_b):
        import jax, jax.numpy as jnp
        import numpy as np
        B, L, C1, C2, K, K_IN = (4, 512, 512, 512, 32, 32)
        BN_EPS = 1e-05

        def _gated_bottleneck(x2d, conv_w, conv_b, gamma, beta, lin_w, lin_b):
            n = x2d.shape[0]
            g = conv_w.shape[0]
            xc = jnp.einsum('ngf,gf->ng', x2d.reshape(n, g, 4), conv_w) + conv_b
            mean = jnp.mean(xc, axis=0)
            var = jnp.mean((xc - mean) ** 2, axis=0)
            xn = (xc - mean) * jax.lax.rsqrt(var + BN_EPS) * gamma + beta
            xa = jax.nn.gelu(xn, approximate=False)
            return xa @ lin_w.T + lin_b
        b, l, c1 = x.shape
        c2 = weight.shape[1]
        x2d = x.reshape(b * l, c1)
        bi = jnp.arange(b)[:, None, None]
        li = jnp.arange(l)[None, :, None]
        score_out = jax.nn.softmax(_gated_bottleneck(x2d, so_conv_w, so_conv_b, so_gamma, so_beta, so_lin_w, so_lin_b).reshape(b, l, c2), axis=-1)
        s_v_out, s_i_out = jax.lax.top_k(score_out, K)
        full = jnp.einsum('blc,co->blo', x, weight)
        out_k = jnp.take_along_axis(full, s_i_out, axis=-1) * s_v_out
        out_branch = jnp.zeros((b, l, c2), x.dtype).at[bi, li, s_i_out].add(out_k)
        score_in = jax.nn.softmax(_gated_bottleneck(x2d, si_conv_w, si_conv_b, si_gamma, si_beta, si_lin_w, si_lin_b).reshape(b, l, c1), axis=-1)
        s_v_in, s_i_in = jax.lax.top_k(score_in, K_IN)
        x_gated = jnp.take_along_axis(x, s_i_in, axis=-1) * s_v_in
        x_sparse = jnp.zeros((b, l, c1), x.dtype).at[bi, li, s_i_in].add(x_gated)
        in_branch = jnp.einsum('blc,co->blo', x_sparse, weight)
        return out_branch + in_branch + bias
    x = L0_attn_x
    x = x + _layernorm(_L0_attn_ref(_layernorm(x, axis=-1), L0_attn_Wq, L0_attn_bq, L0_attn_Wk, L0_attn_bk, L0_attn_Wv, L0_attn_bv, L0_attn_Wo, L0_attn_bo), axis=-1)
    x = x + _layernorm(_L0_ffn_ref(_layernorm(x, axis=-1), L0_ffn_weight, L0_ffn_bias, L0_ffn_so_conv_w, L0_ffn_so_conv_b, L0_ffn_so_gamma, L0_ffn_so_beta, L0_ffn_so_lin_w, L0_ffn_so_lin_b, L0_ffn_si_conv_w, L0_ffn_si_conv_b, L0_ffn_si_gamma, L0_ffn_si_beta, L0_ffn_si_lin_w, L0_ffn_si_lin_b), axis=-1)
    return x

_drawn_inputs = setup_inputs


def setup_inputs(seed=0):
    import zlib

    import numpy as np

    out = dict(_drawn_inputs(seed))
    spreads = {'L0_attn_bq': (0.0, 0.8),
     'L0_attn_bk': (0.0, 0.8),
     'L0_attn_bv': (0.0, 0.1),
     'L0_attn_bo': (0.0, 0.1),
     'L0_ffn_bias': (0.0, 0.1),
     'L0_ffn_so_conv_b': (0.0, 0.8),
     'L0_ffn_so_gamma': (1.0, 0.6),
     'L0_ffn_so_beta': (0.0, 0.8),
     'L0_ffn_so_lin_b': (0.0, 0.8),
     'L0_ffn_si_conv_b': (0.0, 0.8),
     'L0_ffn_si_gamma': (1.0, 0.6),
     'L0_ffn_si_beta': (0.0, 0.8),
     'L0_ffn_si_lin_b': (0.0, 0.8)}
    factors = {'L0_ffn_weight': 3.065,
     'L0_ffn_so_conv_w': 4.731,
     'L0_ffn_so_lin_w': 4.507,
     'L0_ffn_si_conv_w': 4.934,
     'L0_ffn_si_lin_w': 4.665}
    for name, (base, spread) in spreads.items():
        noise = np.random.default_rng([zlib.crc32(name.encode()), seed]).standard_normal(out[name].shape)
        drawn = base * np.exp(spread * noise) if base else spread * noise
        out[name] = jnp.asarray(drawn.astype(out[name].dtype))
    for name, factor in factors.items():
        out[name] = (out[name] * factor).astype(out[name].dtype)
    return out
```

```python
from contextlib import ExitStack

import numpy as np
import concourse.bass as bass
from concourse import mybir

F32 = mybir.dt.float32
F16 = mybir.dt.float16
ALU = mybir.AluOpType
ACT = mybir.ActivationFunctionType
AX = mybir.AxisListType

P = 128
B, S, D = 4, 2048, 512
G = D // 4
C = D // P
TILES = S // P
GROUP = 4
GROUPS = TILES // GROUP
TOPK = 32
EPS = 1e-5
NEG = 10000.0

W_SCALE = 2.0 ** 8
A_SCALE = 2.0 ** 5
P_SCALE = 2.0 ** 13
QKV_DOWN = A_SCALE / (W_SCALE * W_SCALE)
S_SCALE = 1.0 / (A_SCALE * A_SCALE * float(np.sqrt(np.float32(D))))
Y_DOWN = 1.0 / P_SCALE
O_DOWN = 1.0 / (A_SCALE * W_SCALE)
L_DOWN = 1.0 / (A_SCALE * W_SCALE)
FF_SCALE = W_SCALE * W_SCALE
SIDE = 8


def chunks_of(t):
    return t // GROUP + 1


CHUNKS = sum(chunks_of(t) for t in range(TILES))


def chunk_index(t, j):
    return sum(chunks_of(u) for u in range(t)) + j


class Signal:

    def __init__(self, sem, per_round, late=0, step=1):
        self.sem, self.per, self.late, self.step = sem, per_round, late, step

    def prime(self, eng):
        eng.sem_inc(self.sem, (self.per - self.late) * self.step)

    def at(self, r, i):
        return r * (self.per * self.step) + (self.per + i + 1) * self.step


def layer_block(nc, x, wqkvo, bqk, bv, bo, ffw, ffb, linw, linb, convw, chan, ident, negid, mask, out):
    ctx = ExitStack()
    with ctx:
        def sem(name):
            return ctx.enter_context(nc.semaphore(name))

        def sig(name, per, late=0, step=1):
            return Signal(sem(name), per, late, step)

        x1_d = nc.dram_tensor("x1_scratch", [(B + 1) * TILES + GROUP, P, D], F32, kind="Internal").ap()
        h2_d = nc.dram_tensor("h2_scratch", [(B + 1) * TILES, P, D], F32, kind="Internal").ap()
        xc_d = nc.dram_tensor("xc_scratch", [(B + 1) * TILES, P, 2 * P], F32, kind="Internal").ap()
        x_t = x.rearrange("b (t p) d -> (b t) p d", p=P)
        out_t = out.rearrange("b (t p) d -> (b t) p d", p=P)

        psum = ctx.enter_context(nc.psum_tensor("psum", [P, 8, 512], F32))
        T_BANK = [psum[:, n, :] for n in (0, 1)]
        M_BANK = [psum[:, n, :] for n in (2, 3, 4, 5)]
        Y_BANK = [psum[:, n, :] for n in (6, 7)]

        def keep(name, shape, dt):
            return ctx.enter_context(nc.sbuf_tensor(name, shape, dt))
        idn = keep("idn", [P, P], F32)
        chan_s = keep("chan_s", [P, 2, 3], F32)
        bn_all = keep("bn_all", [P, (B + 1) * TILES, 2, 6], F32)
        expo = keep("expo", [P, 8], F32)

        with ExitStack() as actx:
            def sa(name, shape, dt):
                return actx.enter_context(nc.sbuf_tensor(name, shape, dt))
            w_hi = sa("w_hi", [P, 4, C, D], F16)
            w_lo = sa("w_lo", [P, 4, C, D], F16)
            qT = sa("qT", [P, 2, C, S], F16)
            kT = sa("kT", [P, 2, C, S], F16)
            v = sa("v", [P, 2, TILES, D], F16)
            work = sa("work", [P, 7168], F32)
            hT = [work[:, 2048 * n:2048 * (n + 1)].bitcast(F16).rearrange("p (h c n) -> p h c n", h=2, c=C)
                  for n in (0, 1)]
            xg = work[:, 4096:6144].rearrange("p (j n) -> p j n", j=GROUP)
            raw = work[:, 6144:7168].rearrange("p (s n) -> p s n", s=2)
            sS = [work[:, 2048 * n:2048 * (n + 1)] for n in range(3)]
            pT = work[:, 6144:7168].bitcast(F16).rearrange("p (s h n) -> p s h n", s=2, h=2)
            yn = sa("yn", [P, D], F32)
            yT = sa("yT", [P, 2, C, P], F16)
            ob = sa("ob", [P, 2, D], F32)
            xr = sa("xr", [P, 4, D], F32)
            hb = sa("hb", [P, 2, D], F32)
            prod = sa("prod", [P, D], F32)
            xcs = sa("xcs", [P, 2, 2 * P], F32)
            xcT = sa("xcT", [P, 2, 2, P], F32)
            bo_b = sa("bo_b", [P, D], F32)
            bv_b = sa("bv_b", [P, D], F32)
            cw_b = sa("cw_b", [P, 2, D], F32)
            mask_s = sa("mask_s", [P, 512], F32)
            bqk_s = sa("bqk_s", [P, 2, C], F32)
            st1 = sa("st1", [P, GROUP, 6], F32)
            mv1 = sa("mv1", [P, 2, GROUP, 2], F32)
            ve1 = sa("ve1", [P, GROUP], F32)
            rs1 = sa("rs1", [P, 2, GROUP], F32)
            pm = sa("pm", [P, 3, 4], F32)
            nm = sa("nm", [P, 3], F32)
            ssum = sa("ssum", [P, 3], F32)
            rcp = sa("rcp", [P, 2], F32)
            st2 = sa("st2", [P, 6], F32)
            mv2 = sa("mv2", [P, 2, 2], F32)
            ve2 = sa("ve2", [P, 1], F32)
            rs2 = sa("rs2", [P, 2, 2], F32)
            st3 = sa("st3", [P, 6], F32)
            mv3 = sa("mv3", [P, 2, 2], F32)
            ve3 = sa("ve3", [P, 1], F32)
            rs3 = sa("rs3", [P, 2, 1], F32)

        with ExitStack() as bctx:
            def sc(name, shape, dt):
                return bctx.enter_context(nc.sbuf_tensor(name, shape, dt))
            fw = sc("fw", [P, 2, C, D], F16)
            lw = sc("lw", [P, 2, 2, D], F16)
            lb = sc("lb", [2, 2, D], F16)
            lb_raw = sc("lb_raw", [1, 2, D], F32)
            lb_half = sc("lb_half", [1, 2, 2, D], F16)
            ones = sc("ones", [2, P], F16)
            ffb_b = sc("ffb_b", [P, D], F32)
            nid = sc("nid", [P, P], F16)
            wstage = sc("wstage", [P, C, D], F32)
            lstage = sc("lstage", [P, 2, D], F32)
            bn_mv = sc("bn_mv", [P, 2, 2], F32)
            bn_ve = sc("bn_ve", [P, 2], F32)
            bn_sc = sc("bn_sc", [P, 2], F32)
            bn_bi = sc("bn_bi", [P, 2], F32)
            xcg = sc("xcg", [P, 2, GROUP, 2, P], F32)
            xa = sc("xa", [P, GROUP, 2, P], F32)
            xaT = sc("xaT", [P, 2, 2, GROUP, 2, P], F16)
            h2 = sc("h2", [P, 4, D], F32)
            x1 = sc("x1", [P, 4, D], F32)
            h2T = sc("h2T", [P, 2, 2, C, P], F16)
            xsT = sc("xsT", [P, 2, 2, C, P], F16)
            ex = sc("ex", [P, 4, 2, D], F32)
            cut = sc("cut", [P, 2, 2, D], F32)
            rest = sc("rest", [P, 2, 2, D], F32)
            sel = sc("sel", [P, 2, 2, D], F32)
            xs = sc("xs", [P, 2, D], F32)
            zz = sc("zz", [P, 8, D], F32)
            t_in = sc("t_in", [P, 2, D], F32)
            zn = sc("zn", [P, 2, D], F32)
            junk = sc("junk", [P, D], F32)
            m8 = sc("m8", [P, 2, 8], F32)
            e8 = sc("e8", [P, 2, 8], F32)
            c8 = sc("c8", [P, 2, 3, 8], F32)
            nmx = sc("nmx", [P, 2], F32)
            den = sc("den", [P, 2, 2], F32)
            rden = sc("rden", [P, 4, 2], F32)
            zsum = sc("zsum", [P, 2], F32)
            zneg = sc("zneg", [P, 4], F32)
            zsq = sc("zsq", [P, 2], F32)
            zvar = sc("zvar", [P, 1], F32)
            zsc = sc("zsc", [P, 2, 2], F32)

        const_in, w_in, row_out = sem("const_in"), sem("w_in"), sem("row_out")
        setup_dve, setup_act, setup_pool = sem("setup_dve"), sem("setup_act"), sem("setup_pool")
        xg_in = [sig(f"xg_in{j}", GROUPS, step=16) for j in range(GROUP)]
        xr_in = [sig(f"xr_in{j}", TILES // 4, step=16) for j in range(4)]
        x1_out = [sig(f"x1_out{j}", TILES // 4, late=int(j == 3), step=16) for j in range(4)]
        h2_out = [sig(f"h2_out{j}", TILES // 2, late=1 + j, step=16) for j in range(2)]
        xc_out = [sig(f"xc_out{j}", TILES // 2, late=2, step=16) for j in range(2)]
        ln_stat = sig("ln_stat", TILES)
        ln_mv = sig("ln_mv", TILES)
        ln_ve = sig("ln_ve", GROUPS)
        ln_rs = sig("ln_rs", GROUPS)
        hn_ok = sig("hn_ok", TILES)
        T_ITEMS = TILES + CHUNKS + TILES
        t_ps = sig("t_ps", T_ITEMS)
        t_hi = sig("t_hi", T_ITEMS)
        t_lo = sig("t_lo", T_ITEMS)
        kq_ps = sig("kq_ps", 2 * TILES)
        kq_ev = sig("kq_ev", 2 * TILES)
        kq_lo = sig("kq_lo", 2 * TILES)
        v_ps = sig("v_ps", TILES)
        v_ev = sig("v_ev", TILES)
        v_hi = sig("v_hi", TILES)
        v_lo = sig("v_lo", TILES)
        s_ps = sig("s_ps", CHUNKS)
        s_ev = sig("s_ev", CHUNKS)
        nm_ok = sig("nm_ok", TILES)
        p_ok = sig("p_ok", TILES)
        rcp_ok = sig("rcp_ok", TILES)
        y_ps = sig("y_ps", TILES)
        yn_ok = sig("yn_ok", TILES)
        o_ps = sig("o_ps", TILES)
        o_ev = sig("o_ev", TILES)
        relu_ok = sig("relu_ok", TILES)
        st2_ok = sig("st2_ok", TILES, late=1)
        mv2_ok = sig("mv2_ok", TILES, late=1)
        ve2_ok = sig("ve2_ok", TILES, late=1)
        rsd2_ok = sig("rsd2_ok", TILES, late=1)
        rs2_ok = sig("rs2_ok", TILES, late=1)
        n_ok = sig("n_ok", TILES, late=1)
        x1_ok = sig("x1_ok", TILES, late=1)
        st3_ok = sig("st3_ok", TILES, late=2)
        mv3_ok = sig("mv3_ok", TILES, late=2)
        ve3_ok = sig("ve3_ok", TILES, late=2)
        rs3_ok = sig("rs3_ok", TILES, late=2)
        h2_ok = sig("h2_ok", TILES, late=3)
        pr_ok = sig("pr_ok", 2 * TILES, late=6)
        xc_ok = sig("xc_ok", 2 * TILES, late=6)
        x_ps = sig("x_ps", TILES, late=4)
        x_ev = sig("x_ev", TILES, late=4)
        bn_ok = sig("bn_ok", TILES, late=5)
        signals_of = {
            "pe": [t_ps, kq_ps, v_ps, s_ps, y_ps, o_ps, x_ps],
            "act": [t_hi, kq_ev, v_hi, p_ok, yn_ok, relu_ok, n_ok, x_ev],
            "dve": [ln_stat, ln_mv, hn_ok, t_lo, kq_lo, v_ev, v_lo, s_ev, nm_ok, rcp_ok, o_ev, st2_ok,
                    mv2_ok, st3_ok, mv3_ok, h2_ok, pr_ok, xc_ok, bn_ok],
            "pool": [ln_ve, ln_rs, ve2_ok, rsd2_ok, rs2_ok, x1_ok, ve3_ok, rs3_ok],
            "sp": xg_in + xr_in + x1_out + h2_out + xc_out,
        }

        def pe_steps():
            for j in range(GROUP):
                yield ("hT", j)
            for g in range(GROUPS):
                for c in range(C):
                    yield ("k", g, c)
                for c in range(C):
                    yield ("q", g, c)
                    if g + 1 < GROUPS:
                        yield ("hT", GROUP * (g + 1) + c)
                for j in range(GROUP):
                    yield ("v", g, j)
                yield ("x", g - 4)
            for i in range(TILES + 3):
                u, t = i - 2, i - 3
                if 0 <= u < TILES:
                    yield ("pT", u, 0)
                if i < TILES:
                    for j in range(chunks_of(i)):
                        yield ("s", i, j)
                if 0 <= t < TILES:
                    yield ("yT", t)
                if 0 <= u < TILES:
                    for g in range(chunks_of(u)):
                        if g + 1 < chunks_of(u):
                            yield ("pT", u, g + 1)
                        yield ("pv", u, g)
                if 0 <= t < TILES:
                    yield ("o", t)
                if 0 <= i - 7 < TILES - 4:
                    yield ("x", i - 7)

        t_items = [s for s in pe_steps() if s[0] in ("hT", "pT", "yT")]
        m_items = [s for s in pe_steps() if s[0] in ("k", "q", "v", "s", "o", "x")]
        t_place = {s: n for n, s in enumerate(t_items)}
        m_place = {s: n for n, s in enumerate(m_items)}
        assert len(t_items) == T_ITEMS and len(t_items) % 2 == 0 and len(m_items) % 4 == 0

        def t_bank(step):
            return T_BANK[t_place[step] % 2]

        def m_bank(step):
            return M_BANK[m_place[step] % 4]

        def m_freed(step, b):
            kind, *rest = step
            if kind in ("k", "q"):
                return kq_ev, kq_ev.at(b, 8 * rest[0] + 4 * (kind == "q") + rest[1])
            if kind == "v":
                return v_ev, v_ev.at(b, GROUP * rest[0] + rest[1])
            if kind == "s":
                return s_ev, s_ev.at(b, chunk_index(*rest))
            if kind == "o":
                return o_ev, o_ev.at(b, rest[0])
            return x_ev, x_ev.at(b, rest[0])


        passed = sem("passed")

        def wait_apart(eng, signal, value):
            eng.wait_ge(signal.sem, value)
            eng.sem_inc(passed, 1)

        with nc.Block() as block:
            @block.sync
            def _(sp):
                for s in signals_of["sp"]:
                    s.prime(sp)
                for dst, src in ((idn[:], ident), (chan_s[:], chan), (bo_b[:], bo), (bv_b[:], bv), (cw_b[:], convw),
                                 (mask_s[:], mask), (bqk_s[:], bqk)):
                    sp.dma_start(dst, src).then_inc(const_in, 16)
                w_stage = v[:].rearrange("p h t n -> p (h t n)").bitcast(F32).rearrange("p (w c n) -> p w c n", w=4, c=C)
                for n in range(4):
                    sp.dma_start(w_stage[:, n], wqkvo[n].rearrange("(c p) n -> p c n", p=P)).then_inc(w_in, 16)
                sp.wait_ge(setup_pool, 1)
                sp.dma_start(h2_d[TILES - GROUP], hb[:, 0, :]).then_inc(row_out, 16)
                for n in (2, 3):
                    sp.dma_start(x1_d[(B + 1) * TILES + n], hb[:, 0, :]).then_inc(row_out, 16)
                sp.wait_ge(row_out, 16 * 3)

                def load_x(b, g):
                    for j in range(GROUP):
                        last = t_place["hT", GROUP * (g - 1) + j] if g else t_place["pT", TILES - 1, GROUPS - 1] - T_ITEMS
                        sp.wait_ge(t_ps.sem, t_ps.at(b, last))
                        sp.dma_start(xg[:, j, :], x_t[bass.ds(b * TILES + (GROUP * g + j), 1)].rearrange("o p n -> (o p) n")) \
                            .then_inc(xg_in[j].sem, 16)

                def load_residual(b, t):
                    slot = t % 4
                    sp.wait_ge(x1_out[slot].sem, x1_out[slot].at(b, t // 4 - 1))
                    sp.wait_ge(h2_ok.sem, h2_ok.at(b, t - 4))
                    sp.dma_start(xr[:, slot, :], x_t[bass.ds(b * TILES + t, 1)].rearrange("o p n -> (o p) n")) \
                        .then_inc(xr_in[slot].sem, 16)

                def row(d, b, t):
                    return d[bass.ds(b * TILES + (TILES + t), 1)].rearrange("o p n -> (o p) n")

                def store_x1(b, t):
                    sp.wait_ge(x1_ok.sem, x1_ok.at(b, t))
                    sp.dma_start(row(x1_d, b, t), xr[:, t % 4, :]).then_inc(x1_out[t % 4].sem, 16)

                def store_h2(b, t):
                    sp.wait_ge(h2_ok.sem, h2_ok.at(b, t))
                    sp.dma_start(row(h2_d, b, t), hb[:, t % 2, :]).then_inc(h2_out[t % 2].sem, 16)

                def store_xc(b, t):
                    sp.wait_ge(x_ev.sem, x_ev.at(b, t))
                    sp.dma_start(row(xc_d, b, t), xcT[:, t % 2].rearrange("p r n -> p (r n)")) \
                        .then_inc(xc_out[t % 2].sem, 16)

                def late_stores(b, g):
                    if g == 0:
                        store_x1(b, -1)
                    if g < 3:
                        store_h2(b, g - 3)
                    store_xc(b, g - 4)

                with sp.Fori(0, B) as b:
                    load_x(b, 0)
                    for g in range(GROUPS):
                        if g + 1 < GROUPS:
                            load_x(b, g + 1)
                        late_stores(b, g)
                    for i in range(TILES + 3):
                        if 0 <= i - 2 < TILES:
                            load_residual(b, i - 2)
                        if 0 <= i - 4 < TILES:
                            store_x1(b, i - 4)
                        if 0 <= i - 6 < TILES:
                            store_h2(b, i - 6)
                        if 0 <= i - 7 < TILES - 4:
                            store_xc(b, i - 7)
                for g in range(GROUPS):
                    late_stores(B, g)
                for signals, per in ((x1_out, 4), (h2_out, 2), (xc_out, 2)):
                    for n, s in enumerate(signals):
                        sp.wait_ge(s.sem, s.at(B, -1))

            @block.tensor
            def _(pe):
                for s in signals_of["pe"]:
                    s.prime(pe)
                pe.wait_ge(const_in, 16 * 7)
                pe.wait_ge(setup_dve, 1)
                pe.wait_ge(setup_pool, 1)

                def three(outp, n, total, stat, mov):
                    for k, (a, c) in enumerate(((0, 0), (0, 1), (1, 0))):
                        mm = nc.tensor.matmul(outp, stat(a), mov(c), start=(n == 0 and k == 0),
                                              stop=(n == total - 1 and k == 2))
                    return mm

                def take_t(b, step):
                    pe.wait_ge(t_lo.sem, t_lo.at(b, t_place[step] - 2))
                    return t_bank(step)

                def take_m(b, step):
                    n = m_place[step]
                    before = m_items[n - 4]
                    signal, value = m_freed(before, b if n >= 4 else b - 1)
                    pe.wait_ge(signal.sem, value)
                    return m_bank(step)

                def conv_transposes(b, t, bank):
                    pe.wait_ge(xc_ok.sem, xc_ok.at(b, 2 * t + 1))
                    for r in range(2):
                        mm = nc.tensor.transpose(bank[:, P * r:P * (r + 1)], xcs[:, t % 2, P * r:P * (r + 1)], idn[:])
                    mm.then_inc(x_ps.sem, 1)

                with pe.Fori(0, B) as b:
                    for step in pe_steps():
                        kind, *at = step
                        if kind == "hT":
                            t, = at
                            bank = take_t(b, step)
                            pe.wait_ge(hn_ok.sem, hn_ok.at(b, t))
                            for c in range(C):
                                mm = nc.tensor.transpose(bank[:, P * c:P * (c + 1)], xg[:, t % GROUP, P * c:P * (c + 1)], idn[:])
                            mm.then_inc(t_ps.sem, 1)
                        elif kind in ("k", "q"):
                            g, c = at
                            bank = take_m(b, step)
                            if kind == "k" and c == 0:
                                pe.wait_ge(t_lo.sem, t_lo.at(b, t_place["hT", GROUP * g + GROUP - 1]))
                            w, h = (1 if kind == "k" else 0), hT[g % 2]
                            for n in range(C):
                                mm = three(bank, n, C, lambda a: (w_hi, w_lo)[a][:, w, n, P * c:P * (c + 1)], lambda a: h[:, a, n, :])
                            mm.then_inc(kq_ps.sem, 1)
                        elif kind == "v":
                            g, j = at
                            bank, h = take_m(b, step), hT[g % 2]
                            for n in range(C):
                                mm = three(bank, n, C, lambda a: h[:, a, n, P * j:P * (j + 1)], lambda a: (w_hi, w_lo)[a][:, 2, n, :])
                            mm.then_inc(v_ps.sem, 1)
                        elif kind == "s":
                            t, j = at
                            bank = take_m(b, step)
                            if t == 0:
                                pe.wait_ge(kq_lo.sem, kq_lo.at(b, 2 * TILES - 1))
                                pe.wait_ge(v_lo.sem, v_lo.at(b, TILES - 1))
                            w = min(512, P * (t + 1) - 512 * j)
                            for n in range(C):
                                mm = three(bank[:, 0:w], n, C, lambda a: qT[:, a, n, P * t:P * (t + 1)],
                                           lambda a: kT[:, a, n, 512 * j:512 * j + w])
                            mm.then_inc(s_ps.sem, 1)
                        elif kind == "pT":
                            u, g = at
                            bank = take_t(b, step)
                            pe.wait_ge(p_ok.sem, p_ok.at(b, u))
                            for n in range(min(GROUP, u + 1 - GROUP * g)):
                                k = 512 * g + P * n
                                mm = nc.tensor.transpose(bank[:, P * n:P * (n + 1)], sS[u % 3][:, k:k + P], idn[:])
                            mm.then_inc(t_ps.sem, 1)
                        elif kind == "pv":
                            u, g = at
                            if g == 0:
                                pe.wait_ge(yn_ok.sem, yn_ok.at(b, u - 2))
                            pe.wait_ge(t_lo.sem, t_lo.at(b, t_place["pT", u, g]))
                            slot = chunk_index(u, g) % 2
                            for n in range(min(GROUP, u + 1 - GROUP * g)):
                                mm = three(Y_BANK[u % 2], GROUP * g + n, u + 1, lambda a: pT[:, slot, a, P * n:P * (n + 1)],
                                           lambda a: v[:, a, GROUP * g + n, :])
                            if g == chunks_of(u) - 1:
                                mm.then_inc(y_ps.sem, 1)
                        elif kind == "yT":
                            t, = at
                            bank = take_t(b, step)
                            pe.wait_ge(yn_ok.sem, yn_ok.at(b, t))
                            for c in range(C):
                                mm = nc.tensor.transpose(bank[:, P * c:P * (c + 1)], yn[:, P * c:P * (c + 1)], idn[:])
                            mm.then_inc(t_ps.sem, 1)
                        elif kind == "o":
                            t, = at
                            bank = take_m(b, step)
                            pe.wait_ge(t_lo.sem, t_lo.at(b, t_place["yT", t]))
                            for n in range(C):
                                mm = three(bank, n, C, lambda a: yT[:, a, n, :], lambda a: (w_hi, w_lo)[a][:, 3, n, :])
                            mm.then_inc(o_ps.sem, 1)
                        else:
                            t, = at
                            conv_transposes(b, t, take_m(b, step))
                pe.wait_ge(s_ev.sem, s_ev.at(B, -1))
                pe.wait_ge(o_ev.sem, o_ev.at(B, -1))
                for g in range(GROUPS):
                    pe.wait_ge(x_ev.sem, x_ev.at(B, g - 5))
                    conv_transposes(B, g - 4, m_bank(("x", g - 4)))

            @block.scalar
            def _(act):
                for s in signals_of["act"]:
                    s.prime(act)
                w_stage = v[:].rearrange("p h t n -> p (h t n)").bitcast(F32).rearrange("p (w c n) -> p w c n", w=4, c=C)
                act.wait_ge(w_in, 16 * 4)
                for n in range(4):
                    nc.scalar.activation(w_hi[:, n], w_stage[:, n], ACT.Copy, scale=W_SCALE).then_inc(setup_act, 1)
                act.wait_ge(setup_dve, 1)
                act.wait_ge(const_in, 16 * 7)
                act.wait_ge(setup_pool, 1)

                def hi_half(b, step, dst, scale):
                    act.wait_ge(t_ps.sem, t_ps.at(b, t_place[step]))
                    src = t_bank(step)[:, 0:dst.shape[-1]] if len(dst.shape) == 2 else t_bank(step).rearrange("p (c n) -> p c n", c=C)
                    nc.scalar.activation(dst, src, ACT.Copy, scale=scale).then_inc(t_hi.sem, 1)

                def hi_h(b, t):
                    j = t % GROUP
                    hi_half(b, ("hT", t), hT[(t // GROUP) % 2][:, 0, :, P * j:P * (j + 1)], W_SCALE)

                def relu_kq(b, g, kind, c):
                    n = 8 * g + 4 * kind + c
                    step = ("kq"[kind], g, c)
                    act.wait_ge(kq_ps.sem, kq_ps.at(b, n))
                    act.wait_ge(kq_lo.sem, kq_lo.at(b, n - 2))
                    if kind == 0 and c < 2:
                        act.wait_ge(v_lo.sem, v_lo.at(b, GROUP * g - 1))
                    dst, bias = (kT, qT)[kind], bqk_s[:, 1 - kind, c:c + 1]
                    nc.scalar.activation(raw[:, n % 2, :], m_bank(step), ACT.Relu, bias=bias, scale=QKV_DOWN)
                    nc.scalar.activation(dst[:, 0, c, 512 * g:512 * (g + 1)], m_bank(step), ACT.Relu, bias=bias,
                                         scale=QKV_DOWN).then_inc(kq_ev.sem, 1)

                def hi_v(b, t):
                    act.wait_ge(v_ev.sem, v_ev.at(b, t))
                    nc.scalar.activation(v[:, 0, t, :], raw[:, t % 2, :], ACT.Relu).then_inc(v_hi.sem, 1)

                def normed(b, t):
                    act.wait_ge(rs2_ok.sem, rs2_ok.at(b, t))
                    nc.scalar.activation(ob[:, t % 2, :], ob[:, t % 2, :], ACT.Identity, bias=rs2[:, t % 2, 1:2],
                                         scale=rs2[:, t % 2, 0:1]).then_inc(n_ok.sem, 1)

                def conv_out(b, t):
                    act.wait_ge(x_ps.sem, x_ps.at(b, t))
                    act.wait_ge(xc_out[t % 2].sem, xc_out[t % 2].at(b, t // 2 - 1))
                    act.wait_ge(bn_ok.sem, bn_ok.at(b, t - 2))
                    for r in range(2):
                        i = nc.scalar.activation(xcT[:, t % 2, r, :], m_bank(("x", t if t < 12 else t - 16))[:, P * r:P * (r + 1)],
                                                 ACT.Identity, bias=chan_s[:, r, 0:1])
                    i.then_inc(x_ev.sem, 1)

                with act.Fori(0, B) as b:
                    for t in range(GROUP):
                        hi_h(b, t)
                    for g in range(GROUPS):
                        for c in range(C):
                            relu_kq(b, g, 0, c)
                        for c in range(C):
                            relu_kq(b, g, 1, c)
                            if g + 1 < GROUPS:
                                hi_h(b, GROUP * (g + 1) + c)
                        if g == 0:
                            normed(b, -1)
                        for j in range(GROUP):
                            hi_v(b, GROUP * g + j)
                        conv_out(b, g - 4)
                    for i in range(TILES + 3):
                        u, t = i - 2, i - 3
                        if 0 <= u < TILES:
                            groups = chunks_of(u)

                            def hi_p(g):
                                slot = chunk_index(u, g) % 2
                                hi_half(b, ("pT", u, g), pT[:, slot, 0, 0:P * min(GROUP, u + 1 - GROUP * g)], P_SCALE)
                            hi_p(0)
                        if 0 <= t < TILES:
                            hi_half(b, ("yT", t), yT[:, 0], Y_DOWN)
                        if 0 <= u < TILES:
                            for g in range(1, groups):
                                hi_p(g)
                        if i < TILES:
                            w = P * (i + 1)
                            act.wait_ge(nm_ok.sem, nm_ok.at(b, i))
                            nc.scalar.activation(sS[i % 3][:, 0:w], sS[i % 3][:, 0:w], ACT.Exp, bias=nm[:, i % 3:i % 3 + 1],
                                                 accum_out=ssum[:, i % 3:i % 3 + 1]).then_inc(p_ok.sem, 1)
                        if 0 <= i - 4 < TILES:
                            normed(b, i - 4)
                        if 0 <= u < TILES:
                            act.wait_ge(y_ps.sem, y_ps.at(b, u))
                            act.wait_ge(rcp_ok.sem, rcp_ok.at(b, u))
                            nc.scalar.activation(yn[:], Y_BANK[u % 2], ACT.Copy, scale=rcp[:, u % 2:u % 2 + 1]) \
                                .then_inc(yn_ok.sem, 1)
                        if 0 <= t < TILES:
                            act.wait_ge(o_ev.sem, o_ev.at(b, t))
                            nc.scalar.activation(ob[:, t % 2, :], ob[:, t % 2, :], ACT.Relu).then_inc(relu_ok.sem, 1)
                        if 0 <= i - 7 < TILES - 4:
                            conv_out(b, i - 7)
                normed(B, -1)
                for g in range(GROUPS):
                    conv_out(B, g - 4)

            @block.vector
            def _(dve):
                for s in signals_of["dve"]:
                    s.prime(dve)
                w_stage = v[:].rearrange("p h t n -> p (h t n)").bitcast(F32).rearrange("p (w c n) -> p w c n", w=4, c=C)
                dve.wait_ge(const_in, 16 * 7)
                nc.vector.tensor_scalar(bqk_s[:], bqk_s[:], A_SCALE, None, ALU.mult)
                nc.vector.tensor_scalar(bv_b[:], bv_b[:], A_SCALE, None, ALU.mult)
                for n in range(4):
                    dve.wait_ge(setup_act, n + 1)
                    i = nc.vector.scalar_tensor_tensor(w_lo[:, n], w_stage[:, n], W_SCALE, w_hi[:, n], ALU.mult, ALU.subtract)
                i.then_inc(setup_dve, 1)
                dve.wait_ge(setup_dve, 1)
                dve.wait_ge(setup_pool, 1)

                def lo_half(b, step, dst, hi, scale):
                    dve.wait_ge(t_hi.sem, t_hi.at(b, t_place[step]))
                    src = t_bank(step)[:, 0:dst.shape[-1]] if len(dst.shape) == 2 else t_bank(step).rearrange("p (c n) -> p c n", c=C)
                    nc.vector.scalar_tensor_tensor(dst, src, scale, hi, ALU.mult, ALU.subtract).then_inc(t_lo.sem, 1)

                def lo_h(b, t):
                    j, h = t % GROUP, hT[(t // GROUP) % 2]
                    lo_half(b, ("hT", t), h[:, 1, :, P * j:P * (j + 1)], h[:, 0, :, P * j:P * (j + 1)], W_SCALE)

                def ln_stats(b, g):
                    for j in range(GROUP):
                        dve.wait_ge(xg_in[j].sem, xg_in[j].at(b, g))
                        nc.vector.bn_stats(st1[:, j, :], xg[:, j, :]).then_inc(ln_stat.sem, 1)
                    for j in range(GROUP):
                        wait_apart(dve, ln_stat, ln_stat.at(b, GROUP * g + j))
                        nc.vector.bn_aggr(mv1[:, g % 2, j, :], st1[:, j, :]).then_inc(ln_mv.sem, 1)

                def ln_norm(b, g):
                    dve.wait_ge(ln_rs.sem, ln_rs.at(b, g))
                    for j in range(GROUP):
                        nc.vector.tensor_scalar(xg[:, j, :], xg[:, j, :], mv1[:, g % 2, j, 0:1], rs1[:, g % 2, j:j + 1],
                                                ALU.subtract, ALU.mult).then_inc(hn_ok.sem, 1)

                def lo_kq(b, g, kind, c):
                    n = 8 * g + 4 * kind + c
                    dst = (kT, qT)[kind][:, :, c, 512 * g:512 * (g + 1)]
                    dve.wait_ge(kq_ev.sem, kq_ev.at(b, n))
                    nc.vector.tensor_tensor(dst[:, 1], raw[:, n % 2, :], dst[:, 0], ALU.subtract).then_inc(kq_lo.sem, 1)

                def bias_v(b, g, j):
                    t = GROUP * g + j
                    dve.wait_ge(v_ps.sem, v_ps.at(b, t))
                    if j < 2:
                        dve.wait_ge(kq_lo.sem, kq_lo.at(b, 8 * g + 7))
                    else:
                        dve.wait_ge(v_lo.sem, v_lo.at(b, t - 2))
                    nc.vector.scalar_tensor_tensor(raw[:, t % 2, :], m_bank(("v", g, j)), QKV_DOWN, bv_b[:], ALU.mult, ALU.add) \
                        .then_inc(v_ev.sem, 1)

                def lo_v(b, t):
                    dve.wait_ge(v_hi.sem, v_hi.at(b, t))
                    nc.vector.scalar_tensor_tensor(v[:, 1, t, :], raw[:, t % 2, :], 0.0, v[:, 0, t, :], ALU.max, ALU.subtract) \
                        .then_inc(v_lo.sem, 1)

                def attention_stats(b, t):
                    dve.wait_ge(relu_ok.sem, relu_ok.at(b, t))
                    nc.vector.bn_stats(st2[:], ob[:, t % 2, :]).then_inc(st2_ok.sem, 1)
                    wait_apart(dve, st2_ok, st2_ok.at(b, t))
                    nc.vector.bn_aggr(mv2[:, t % 2, :], st2[:]).then_inc(mv2_ok.sem, 1)

                def residual_stats(b, t):
                    dve.wait_ge(x1_ok.sem, x1_ok.at(b, t))
                    nc.vector.bn_stats(st3[:], xr[:, t % 4, :]).then_inc(st3_ok.sem, 1)
                    wait_apart(dve, st3_ok, st3_ok.at(b, t))
                    nc.vector.bn_aggr(mv3[:, t % 2, :], st3[:]).then_inc(mv3_ok.sem, 1)

                def second_norm(b, t):
                    dve.wait_ge(rs3_ok.sem, rs3_ok.at(b, t))
                    dve.wait_ge(h2_out[t % 2].sem, h2_out[t % 2].at(b, t // 2 - 1))
                    dve.wait_ge(xc_ok.sem, xc_ok.at(b, 2 * t - 3))
                    nc.vector.tensor_scalar(hb[:, t % 2, :], xr[:, t % 4, :], mv3[:, t % 2, 0:1], rs3[:, t % 2, 0:1],
                                            ALU.subtract, ALU.mult).then_inc(h2_ok.sem, 1)
                    for r in range(2):
                        dve.wait_ge(h2_ok.sem, h2_ok.at(b, t))
                        dve.wait_ge(xc_ok.sem, xc_ok.at(b, 2 * t + r - 1))
                        nc.vector.tensor_tensor(prod[:], hb[:, t % 2, :], cw_b[:, r, :], ALU.mult).then_inc(pr_ok.sem, 1)
                        dve.wait_ge(pr_ok.sem, pr_ok.at(b, 2 * t + r))
                        dve.wait_ge(x_ps.sem, x_ps.at(b, t - 2))
                        nc.vector.tensor_reduce(xcs[:, t % 2, P * r:P * (r + 1)], prod[:].rearrange("p (g f) -> p g f", f=4),
                                                AX.X, ALU.add).then_inc(xc_ok.sem, 1)

                def conv_stats(b, t):
                    for r in range(2):
                        wait_apart(dve, x_ev, x_ev.at(b, t))
                        i = nc.vector.bn_stats(bn_all[:, bass.ds(b * TILES + (TILES + t), 1), r, :].rearrange("p o s -> p (o s)"),
                                               xcT[:, t % 2, r, :])
                    i.then_inc(bn_ok.sem, 1)

                def late_tiles(b, g):
                    if g < 3:
                        second_norm(b, g - 3)
                    if g < 2:
                        residual_stats(b, g - 2)
                    if g == 0:
                        attention_stats(b, -1)
                    conv_stats(b, g - 5)

                with dve.Fori(0, B) as b:
                    ln_stats(b, 0)
                    ln_norm(b, 0)
                    for t in range(GROUP):
                        lo_h(b, t)
                    for g in range(GROUPS):
                        if g + 1 < GROUPS:
                            ln_stats(b, g + 1)
                        for c in range(C):
                            lo_kq(b, g, 0, c)
                        if g + 1 < GROUPS:
                            ln_norm(b, g + 1)
                        for c in range(C):
                            lo_kq(b, g, 1, c)
                            if g + 1 < GROUPS:
                                lo_h(b, GROUP * (g + 1) + c)
                        late_tiles(b, g)
                        bias_v(b, g, 0)
                        for j in range(1, GROUP):
                            bias_v(b, g, j)
                            lo_v(b, GROUP * g + j - 1)
                        lo_v(b, GROUP * g + GROUP - 1)
                    conv_stats(b, -1)
                    for i in range(TILES + 3):
                        u, t = i - 2, i - 3
                        if 0 <= u < TILES:
                            def lo_p(g):
                                d = pT[:, chunk_index(u, g) % 2, :, 0:P * min(GROUP, u + 1 - GROUP * g)]
                                lo_half(b, ("pT", u, g), d[:, 1], d[:, 0], P_SCALE)
                            lo_p(0)
                        if i < TILES:
                            slot = i % 3
                            for j in range(chunks_of(i)):
                                w, n = min(512, P * (i + 1) - 512 * j), chunk_index(i, j)
                                src, dst = m_bank(("s", i, j))[:, 0:w], sS[slot][:, 512 * j:512 * j + w]
                                wait_apart(dve, s_ps, s_ps.at(b, n))
                                if j + 1 < chunks_of(i):
                                    nc.vector.tensor_scalar(dst, src, S_SCALE, None, ALU.mult, ALU.max,
                                                            accum_out=pm[:, slot, j:j + 1]).then_inc(s_ev.sem, 1)
                                else:
                                    nc.vector.tensor_tensor_reduce(out=dst, in0=src, in1=mask_s[:, 512 - w:512], scale=S_SCALE,
                                                                   scalar=-3e38, op0=ALU.add, op1=ALU.max,
                                                                   accum_out=pm[:, slot, j:j + 1]).then_inc(s_ev.sem, 1)
                            dve.wait_ge(s_ev.sem, s_ev.at(b, chunk_index(i, chunks_of(i) - 1)))
                            nc.vector.tensor_reduce(nm[:, slot:slot + 1], pm[:, slot, 0:chunks_of(i)], AX.X, ALU.max,
                                                    negate=True).then_inc(nm_ok.sem, 1)
                        if 0 <= t < TILES:
                            lo_half(b, ("yT", t), yT[:, 1], yT[:, 0], Y_DOWN)
                        if 0 <= u < TILES:
                            for g in range(1, chunks_of(u)):
                                lo_p(g)
                            dve.wait_ge(p_ok.sem, p_ok.at(b, u))
                            nc.vector.reciprocal(rcp[:, u % 2:u % 2 + 1], ssum[:, u % 3:u % 3 + 1]).then_inc(rcp_ok.sem, 1)
                        if 0 <= i - 6 < TILES:
                            second_norm(b, i - 6)
                        if 0 <= i - 5 < TILES:
                            residual_stats(b, i - 5)
                        if 0 <= i - 4 < TILES:
                            attention_stats(b, i - 4)
                        if 0 <= t < TILES:
                            dve.wait_ge(o_ps.sem, o_ps.at(b, t))
                            dve.wait_ge(x1_ok.sem, x1_ok.at(b, t - 2))
                            nc.vector.scalar_tensor_tensor(ob[:, t % 2, :], m_bank(("o", t)), O_DOWN, bo_b[:], ALU.mult, ALU.add) \
                                .then_inc(o_ev.sem, 1)
                        if 0 <= i - 8 < TILES:
                            conv_stats(b, i - 8)
                for g in range(GROUPS):
                    late_tiles(B, g)
                conv_stats(B, -1)
                dve.wait_ge(bn_ok.sem, bn_ok.at(B, -1))

            @block.gpsimd
            def _(pool):
                for s in signals_of["pool"]:
                    s.prime(pool)
                for a in (ob, xr, hb, xcs, xcT, mv2, mv3, rs2, rs3, bn_all):
                    nc.gpsimd.memset(a[:], 0.0)
                nc.gpsimd.memset(expo[:], -0.5).then_inc(setup_pool, 1)
                pool.wait_ge(setup_pool, 1)

                def ln_scale(b, g):
                    wait_apart(pool, ln_mv, ln_mv.at(b, GROUP * g + GROUP - 1))
                    nc.gpsimd.tensor_scalar(ve1[:], mv1[:, g % 2, :, 1], EPS, None, ALU.add).then_inc(ln_ve.sem, 1)
                    pool.wait_ge(ln_ve.sem, ln_ve.at(b, g))
                    nc.gpsimd.tensor_tensor(rs1[:, g % 2, :], ve1[:], expo[:, 0:GROUP], ALU.pow).then_inc(ln_rs.sem, 1)

                def attention_scale(b, t):
                    m = mv2[:, t % 2, :]
                    wait_apart(pool, mv2_ok, mv2_ok.at(b, t))
                    nc.gpsimd.tensor_scalar(ve2[:], m[:, 1:2], EPS, None, ALU.add).then_inc(ve2_ok.sem, 1)
                    pool.wait_ge(ve2_ok.sem, ve2_ok.at(b, t))
                    nc.gpsimd.tensor_tensor(rs2[:, t % 2, 0:1], ve2[:], expo[:, 0:1], ALU.pow).then_inc(rsd2_ok.sem, 1)
                    wait_apart(pool, rsd2_ok, rsd2_ok.at(b, t))
                    nc.gpsimd.tensor_scalar(rs2[:, t % 2, 1:2], m[:, 0:1], rs2[:, t % 2, 0:1], -1.0, ALU.mult, ALU.mult) \
                        .then_inc(rs2_ok.sem, 1)

                def residual(b, t):
                    pool.wait_ge(n_ok.sem, n_ok.at(b, t))
                    pool.wait_ge(xr_in[t % 4].sem, xr_in[t % 4].at(b, t // 4))
                    nc.gpsimd.tensor_tensor(xr[:, t % 4, :], ob[:, t % 2, :], xr[:, t % 4, :], ALU.add).then_inc(x1_ok.sem, 1)

                def second_scale(b, t):
                    wait_apart(pool, mv3_ok, mv3_ok.at(b, t))
                    nc.gpsimd.tensor_scalar(ve3[:], mv3[:, t % 2, 1:2], EPS, None, ALU.add).then_inc(ve3_ok.sem, 1)
                    pool.wait_ge(ve3_ok.sem, ve3_ok.at(b, t))
                    nc.gpsimd.tensor_tensor(rs3[:, t % 2, :], ve3[:], expo[:, 0:1], ALU.pow).then_inc(rs3_ok.sem, 1)

                def late_tiles(b, g):
                    if g < 2:
                        second_scale(b, g - 2)
                    if g == 0:
                        attention_scale(b, -1)
                        residual(b, -1)

                with pool.Fori(0, B) as b:
                    ln_scale(b, 0)
                    for g in range(GROUPS):
                        if g + 1 < GROUPS:
                            ln_scale(b, g + 1)
                        late_tiles(b, g)
                    for i in range(TILES + 3):
                        if 0 <= i - 5 < TILES:
                            second_scale(b, i - 5)
                        if 0 <= i - 4 < TILES:
                            attention_scale(b, i - 4)
                            residual(b, i - 4)
                for g in range(GROUPS):
                    late_tiles(B, g)

        R = B * TILES // SIDE

        def sig_b(name, per, late=0, step=1):
            return Signal(sem("b_" + name), per, late, step)

        LAG_IN, LAG_Z, LAG_STAT, LAG_NORM, LAG_OUT = 2, 3, 4, 5, 6
        TOP_STEPS = 2 * (2 * (TOPK // 8) - 1)
        setup_b = {e: sem("setup_b_" + e) for e in ("in", "act", "dve", "pool", "lb")}
        xc_in = [sig_b(f"xc_in{n}", 1, step=16) for n in range(2)]
        h2_in = [sig_b(f"h2_in{n}", SIDE // 4, step=16) for n in range(4)]
        x1_in = [sig_b(f"x1_in{n}", SIDE // 4, late=int(n >= 2), step=16) for n in range(4)]
        out_st = [sig_b(f"out_st{n}", SIDE // 2, late=LAG_OUT // 2, step=16) for n in range(2)]
        gelu_ok = sig_b("gelu_ok", 2)
        xa_hi = sig_b("xa_hi", 2)
        xa_lo = sig_b("xa_lo", 2)
        lg_ps = sig_b("lg_ps", 2 * SIDE)
        mx_ok = sig_b("mx_ok", 2 * SIDE)
        nmx_ok = sig_b("nmx_ok", 2 * SIDE)
        e8_ok = sig_b("e8_ok", 2 * SIDE)
        ex_ok = sig_b("ex_ok", 2 * SIDE)
        top_ok = sig_b("top_ok", TOP_STEPS * SIDE)
        rden_ok = sig_b("rden_ok", SIDE)
        sel_ok = sig_b("sel_ok", 2 * SIDE, late=2)
        xs_ok = sig_b("xs_ok", SIDE, late=1)
        hT_ps = sig_b("hT_ps", SIDE)
        hT_hi = sig_b("hT_hi", SIDE)
        hm_ps = sig_b("hm_ps", SIDE)
        hT_lo = sig_b("hT_lo", SIDE)
        xT_ps = sig_b("xT_ps", SIDE, late=1)
        xT_hi = sig_b("xT_hi", SIDE, late=1)
        xm_ps = sig_b("xm_ps", SIDE, late=1)
        xT_lo = sig_b("xT_lo", SIDE, late=1)
        full_ps = sig_b("full_ps", SIDE, late=1)
        tf_ok = sig_b("tf_ok", SIDE, late=1)
        t1_ok = sig_b("t1_ok", SIDE, late=1)
        in_ps = sig_b("in_ps", SIDE, late=LAG_IN)
        tin_ok = sig_b("tin_ok", SIDE, late=LAG_IN)
        z0_ok = sig_b("z0_ok", SIDE, late=LAG_Z)
        z_ok = sig_b("z_ok", SIDE, late=LAG_Z)
        zsum_ok = sig_b("zsum_ok", SIDE, late=LAG_STAT)
        zneg_ok = sig_b("zneg_ok", SIDE, late=LAG_STAT)
        zsq_ok = sig_b("zsq_ok", SIDE, late=LAG_STAT)
        zvar_ok = sig_b("zvar_ok", SIDE, late=LAG_NORM)
        zrs_ok = sig_b("zrs_ok", SIDE, late=LAG_NORM)
        zsc_ok = sig_b("zsc_ok", SIDE, late=LAG_NORM)
        zn_ok = sig_b("zn_ok", SIDE, late=LAG_NORM)
        out_ok = sig_b("out_ok", SIDE, late=LAG_OUT)
        signals_b = {
            "sp": xc_in + h2_in + x1_in + out_st,
            "pe": [lg_ps, hT_ps, hm_ps, xT_ps, xm_ps, full_ps, in_ps],
            "act": [gelu_ok, xa_hi, nmx_ok, e8_ok, ex_ok, hT_hi, hT_lo, xT_hi, xT_lo, tf_ok, tin_ok, zsum_ok,
                    zneg_ok, zsq_ok, zn_ok],
            "dve": [xa_lo, mx_ok, top_ok, rden_ok],
            "pool": [sel_ok, xs_ok, t1_ok, z0_ok, z_ok, zvar_ok, zrs_ok, zsc_ok, out_ok],
        }
        L_BANK = [psum[:, n, :] for n in (0, 1)]
        HT_BANK, XT_BANK = psum[:, 2, :], psum[:, 3, :]
        F_BANK = [psum[:, n, :] for n in (4, 5)]
        I_BANK = [psum[:, n, :] for n in (6, 7)]
        OUT, IN = 0, 1

        def tile_row(r, n):
            return r * -SIDE + (B * TILES - GROUP - GROUP * (n // GROUP) + n % GROUP)

        with nc.Block() as block:
            @block.sync
            def _(sp):
                for s in signals_b["sp"]:
                    s.prime(sp)
                sp.dma_start(wstage[:], ffw.rearrange("(c p) n -> p c n", p=P)).then_inc(setup_b["in"], 16)
                sp.dma_start(lstage[:], linw).then_inc(setup_b["in"], 16)
                sp.dma_start(lb_raw[:], linb).then_inc(setup_b["in"], 16)
                sp.dma_start(ffb_b[:], ffb).then_inc(setup_b["in"], 16)
                sp.dma_start(nid[:], negid).then_inc(setup_b["in"], 16)

                def load_conv(r, side):
                    if side < 2:
                        sp.wait_ge(gelu_ok.sem, gelu_ok.at(r, side - 2))
                    else:
                        sp.wait_ge(gelu_ok.sem, gelu_ok.at(r, 0))
                    rows = xc_d[bass.ds(tile_row(r, GROUP * side) + TILES, GROUP)].rearrange("t p n -> p t n")
                    sp.dma_start(xcg[:, side % 2].rearrange("p t r n -> p t (r n)"), rows).then_inc(xc_in[side % 2].sem, 16)

                def load_h2(r, n):
                    sp.wait_ge(xs_ok.sem, xs_ok.at(r, n - 4))
                    sp.wait_ge(hT_ps.sem, hT_ps.at(r, n - 4))
                    sp.dma_start(h2[:, n % 4, :], h2_d[bass.ds(tile_row(r, n) + TILES, 1)].rearrange("o p n -> (o p) n")) \
                        .then_inc(h2_in[n % 4].sem, 16)

                def load_x1(r, n):
                    sp.wait_ge(out_ok.sem, out_ok.at(r, n - 4))
                    sp.dma_start(x1[:, n % 4, :], x1_d[bass.ds(tile_row(r, n) + TILES, 1)].rearrange("o p n -> (o p) n")) \
                        .then_inc(x1_in[n % 4].sem, 16)

                def store(r, n):
                    sp.wait_ge(out_ok.sem, out_ok.at(r, n))
                    sp.dma_start(out[bass.ds(tile_row(r, n), 1)].rearrange("o p n -> (o p) n"), zn[:, n % 2, :]) \
                        .then_inc(out_st[n % 2].sem, 16)

                load_conv(0, 0)
                sp.wait_ge(setup_b["pool"], 1)
                sp.wait_ge(setup_b["dve"], 1)
                sp.wait_ge(setup_b["act"], 3)
                sp.wait_ge(setup_b["dve"], 4)
                for a in range(2):
                    sp.dma_start(lb[a:a + 1], lb_half[:, a]).then_inc(setup_b["lb"], 16)
                load_h2(0, 0)
                with sp.Fori(0, R) as r:
                    for n in range(SIDE):
                        if n == 0:
                            load_conv(r, 1)
                        if n == GROUP:
                            load_conv(r, 2)
                        load_h2(r, n + 1)
                        load_x1(r, n - 2)
                        store(r, n - LAG_OUT)
                for n in range(LAG_OUT):
                    if n < 2:
                        load_x1(R, n - 2)
                    store(R, n - LAG_OUT)
                sp.wait_ge(h2_in[0].sem, h2_in[0].at(R, 0))
                for s in out_st:
                    sp.wait_ge(s.sem, s.at(R, -1))

            @block.tensor
            def _(pe):
                for s in signals_b["pe"]:
                    s.prime(pe)
                pe.wait_ge(setup_b["in"], 16 * 5)
                pe.wait_ge(setup_b["dve"], 4)
                pe.wait_ge(setup_b["pool"], 1)
                pe.wait_ge(setup_b["lb"], 32)

                def three(outp, n, total, stat, mov, fresh=True):
                    for k, (a, c) in enumerate(((0, 0), (0, 1), (1, 0))):
                        mm = nc.tensor.matmul(outp, stat(a), mov(c), start=(fresh and n == 0 and k == 0),
                                              stop=(n == total - 1 and k == 2))
                    return mm

                def logits(r, n):
                    group, j = (n // GROUP) % 2, n % GROUP
                    pe.wait_ge(xa_lo.sem, xa_lo.at(r, n // GROUP))
                    for s in range(2):
                        pe.wait_ge(ex_ok.sem, ex_ok.at(r, 2 * n - 2 + s))
                        nc.tensor.matmul(L_BANK[s], ones[:], lb[:, s, :], start=True, stop=False)
                        three(L_BANK[s], 0, 1, lambda a: xaT[:, group, a, j, s, :], lambda a: lw[:, s, a, :],
                              fresh=False).then_inc(lg_ps.sem, 1)

                def transposed(src, bank, signal):
                    for c in range(C):
                        mm = nc.tensor.matmul(bank[:, P * c:P * (c + 1)], src[:, P * c:P * (c + 1)], idn[:],
                                              is_transpose=True, start=(c == 0), stop=(c == C - 1), skip_group_check=True)
                    mm.then_inc(signal.sem, 1)

                def less_hi(bank, hi, signal):
                    nc.tensor.matmul(bank, nid[:], hi.rearrange("p c n -> p (c n)"), start=False, stop=True,
                                     skip_group_check=True).then_inc(signal.sem, 1)

                def product(bank, pair, signal):
                    for c in range(C):
                        mm = three(bank, c, C, lambda a: pair[:, a, c, :], lambda a: fw[:, a, c, :])
                    mm.then_inc(signal.sem, 1)

                def step(r, n, tail=False):
                    def due(lag):
                        return not tail or n - lag < 0
                    if not tail:
                        logits(r, n + 1)
                        pe.wait_ge(h2_in[n % 4].sem, h2_in[n % 4].at(r, n // 4))
                        pe.wait_ge(hT_lo.sem, hT_lo.at(r, n - 1))
                        transposed(h2[:, n % 4, :], HT_BANK, hT_ps)
                    m = n - 1
                    if due(1):
                        pe.wait_ge(hT_lo.sem, hT_lo.at(r, m))
                        pe.wait_ge(tf_ok.sem, tf_ok.at(r, m - 2))
                        product(F_BANK[m % 2], h2T[:, m % 2], full_ps)
                    if not tail:
                        pe.wait_ge(hT_hi.sem, hT_hi.at(r, n))
                        less_hi(HT_BANK, h2T[:, n % 2, 0], hm_ps)
                    if due(1):
                        pe.wait_ge(xs_ok.sem, xs_ok.at(r, m))
                        pe.wait_ge(xT_lo.sem, xT_lo.at(r, m - 1))
                        transposed(xs[:, m % 2, :], XT_BANK, xT_ps)
                    if due(LAG_IN):
                        k = n - LAG_IN
                        pe.wait_ge(xT_lo.sem, xT_lo.at(r, k))
                        pe.wait_ge(tin_ok.sem, tin_ok.at(r, k - 2))
                        product(I_BANK[k % 2], xsT[:, k % 2], in_ps)
                    if due(1):
                        pe.wait_ge(xT_hi.sem, xT_hi.at(r, m))
                        less_hi(XT_BANK, xsT[:, m % 2, 0], xm_ps)

                logits(0, 0)
                with pe.Fori(0, R) as r:
                    for n in range(SIDE):
                        step(r, n)
                for n in range(LAG_OUT):
                    step(R, n, tail=True)

            @block.scalar
            def _(act):
                for s in signals_b["act"]:
                    s.prime(act)
                act.wait_ge(setup_b["in"], 16 * 5)
                nc.scalar.activation(fw[:, 0], wstage[:], ACT.Copy, scale=W_SCALE).then_inc(setup_b["act"], 1)
                nc.scalar.activation(lw[:, :, 0, :], lstage[:], ACT.Copy, scale=W_SCALE).then_inc(setup_b["act"], 1)
                nc.scalar.activation(lb_half[:, 0], lb_raw[:], ACT.Copy, scale=W_SCALE).then_inc(setup_b["act"], 1)
                act.wait_ge(setup_b["pool"], 6)
                act.wait_ge(setup_b["dve"], 4)

                def gelu(r, side):
                    slot = side % 2
                    act.wait_ge(xc_in[slot].sem, xc_in[slot].at(r, side // 2))
                    act.wait_ge(xa_lo.sem, xa_lo.at(r, side - 1))
                    for s in range(2):
                        i = nc.scalar.activation(xa[:, :, s, :], xcg[:, slot, :, s, :], ACT.Gelu, bias=bn_bi[:, s:s + 1],
                                                 scale=bn_sc[:, s:s + 1])
                    i.then_inc(gelu_ok.sem, 1)
                    act.wait_ge(gelu_ok.sem, gelu_ok.at(r, side))
                    act.wait_ge(lg_ps.sem, lg_ps.at(r, 2 * (GROUP * (side - 1)) - 1))
                    nc.scalar.activation(xaT[:, slot, 0].rearrange("p t s n -> p (t s n)"),
                                         xa[:].rearrange("p t s n -> p (t s n)"), ACT.Copy, scale=A_SCALE).then_inc(xa_hi.sem, 1)

                def exponentials(r, n):
                    for s in range(2):
                        i = 2 * n + s
                        act.wait_ge(mx_ok.sem, mx_ok.at(r, i))
                        nc.scalar.activation(nmx[:, s:s + 1], m8[:, s, 0:1], ACT.Copy, scale=-L_DOWN).then_inc(nmx_ok.sem, 1)
                    for s in range(2):
                        i = 2 * n + s
                        act.wait_ge(nmx_ok.sem, nmx_ok.at(r, i))
                        nc.scalar.activation(e8[:, s, :], m8[:, s, :], ACT.Exp, bias=nmx[:, s:s + 1], scale=L_DOWN) \
                            .then_inc(e8_ok.sem, 1)
                        act.wait_ge(sel_ok.sem, sel_ok.at(r, i - 8))
                        nc.scalar.activation(ex[:, n % 4, s, :], L_BANK[s], ACT.Exp, bias=nmx[:, s:s + 1], scale=L_DOWN,
                                             accum_out=den[:, n % 2, s:s + 1]).then_inc(ex_ok.sem, 1)

                def half(r, k, before, bank, dst, after):
                    act.wait_ge(before.sem, before.at(r, k))
                    nc.scalar.activation(dst, bank.rearrange("p (c n) -> p c n", c=C), ACT.Copy, scale=W_SCALE) \
                        .then_inc(after.sem, 1)

                def step(r, n, tail=False):
                    def due(lag):
                        return not tail or n - lag < 0
                    if not tail:
                        half(r, n, hT_ps, HT_BANK, h2T[:, n % 2, 0], hT_hi)
                    if due(1):
                        k = n - 1
                        act.wait_ge(full_ps.sem, full_ps.at(r, k))
                        act.wait_ge(rden_ok.sem, rden_ok.at(r, k))
                        act.wait_ge(zn_ok.sem, zn_ok.at(r, k - 8))
                        nc.scalar.activation(zz[:, k % 8, :], F_BANK[k % 2], ACT.Copy, scale=rden[:, k % 4, OUT:OUT + 1]) \
                            .then_inc(tf_ok.sem, 1)
                    if not tail:
                        half(r, n, hm_ps, HT_BANK, h2T[:, n % 2, 1], hT_lo)
                    if due(1):
                        half(r, n - 1, xT_ps, XT_BANK, xsT[:, (n - 1) % 2, 0], xT_hi)
                    if not tail:
                        exponentials(r, n + 1)
                    if due(LAG_IN):
                        k = n - LAG_IN
                        act.wait_ge(in_ps.sem, in_ps.at(r, k))
                        act.wait_ge(z0_ok.sem, z0_ok.at(r, k - 2))
                        nc.scalar.activation(t_in[:, k % 2, :], I_BANK[k % 2], ACT.Copy, scale=rden[:, k % 4, IN:IN + 1]) \
                            .then_inc(tin_ok.sem, 1)
                    if due(1):
                        half(r, n - 1, xm_ps, XT_BANK, xsT[:, (n - 1) % 2, 1], xT_lo)
                    if due(LAG_STAT):
                        k = n - LAG_STAT
                        z = zz[:, k % 8, :]
                        act.wait_ge(z_ok.sem, z_ok.at(r, k))
                        act.wait_ge(zsq_ok.sem, zsq_ok.at(r, k - 1))
                        nc.scalar.activation(junk[:], z, ACT.Copy, accum_out=zsum[:, k % 2:k % 2 + 1]).then_inc(zsum_ok.sem, 1)
                        act.wait_ge(zsum_ok.sem, zsum_ok.at(r, k))
                        nc.scalar.activation(zneg[:, k % 4:k % 4 + 1], zsum[:, k % 2:k % 2 + 1], ACT.Copy, scale=-1.0 / D) \
                            .then_inc(zneg_ok.sem, 1)
                        act.wait_ge(zneg_ok.sem, zneg_ok.at(r, k))
                        nc.scalar.activation(junk[:], z, ACT.Square, bias=zneg[:, k % 4:k % 4 + 1],
                                             accum_out=zsq[:, k % 2:k % 2 + 1]).then_inc(zsq_ok.sem, 1)
                    if due(LAG_NORM):
                        k = n - LAG_NORM
                        act.wait_ge(zsc_ok.sem, zsc_ok.at(r, k))
                        act.wait_ge(out_st[k % 2].sem, out_st[k % 2].at(r, k // 2 - 1))
                        nc.scalar.activation(zn[:, k % 2, :], zz[:, k % 8, :], ACT.Identity, bias=zsc[:, k % 2, 1:2],
                                             scale=zsc[:, k % 2, 0:1]).then_inc(zn_ok.sem, 1)
                    if not tail and n == 1:
                        gelu(r, 1)
                    if not tail and n == GROUP + 1:
                        gelu(r, 2)

                gelu(0, 0)
                exponentials(0, 0)
                with act.Fori(0, R) as r:
                    for n in range(SIDE):
                        step(r, n)
                for n in range(LAG_OUT):
                    step(R, n, tail=True)

            @block.vector
            def _(dve):
                for s in signals_b["dve"]:
                    s.prime(dve)
                for a in (ex, rest, h2T, xsT, zn):
                    nc.vector.memset(a[:], 0.0)
                nc.vector.memset(ones[:], A_SCALE)
                for s in range(2):
                    i = nc.vector.bn_aggr(bn_mv[:, s, :], bn_all[:, TILES:, s, :])
                i.then_inc(setup_b["dve"], 1)
                dve.wait_ge(setup_b["in"], 16 * 5)
                nc.vector.tensor_scalar(ffb_b[:], ffb_b[:], FF_SCALE, None, ALU.mult)
                for n, (dst, src, hi) in enumerate(((fw[:, 1], wstage[:], fw[:, 0]), (lw[:, :, 1, :], lstage[:], lw[:, :, 0, :]),
                                                    (lb_half[:, 1], lb_raw[:], lb_half[:, 0]))):
                    dve.wait_ge(setup_b["act"], n + 1)
                    nc.vector.scalar_tensor_tensor(dst, src, W_SCALE, hi, ALU.mult, ALU.subtract).then_inc(setup_b["dve"], 1)
                dve.wait_ge(setup_b["pool"], 1)

                def gelu_lo(r, side):
                    dve.wait_ge(xa_hi.sem, xa_hi.at(r, side))
                    hi, lo = (xaT[:, side % 2, a].rearrange("p t s n -> p (t s n)") for a in range(2))
                    nc.vector.scalar_tensor_tensor(lo, xa[:].rearrange("p t s n -> p (t s n)"), A_SCALE, hi, ALU.mult,
                                                   ALU.subtract).then_inc(xa_lo.sem, 1)

                def largest(r, n):
                    for s in range(2):
                        wait_apart(dve, lg_ps, lg_ps.at(r, 2 * n + s))
                        nc.vector.max(m8[:, s, :], L_BANK[s]).then_inc(mx_ok.sem, 1)

                def step(r, n):
                    first = TOP_STEPS * n

                    def remove(k, s, dst, eight, src):
                        if k == 0:
                            dve.wait_ge(ex_ok.sem, ex_ok.at(r, 2 * n + s))
                        if k == 6:
                            dve.wait_ge(sel_ok.sem, sel_ok.at(r, 2 * (n - 2) + 1))
                        wait_apart(dve, top_ok, top_ok.at(r, first + 2 * k + s - 2))
                        nc.vector.match_replace(dst, eight, src, 0.0).then_inc(top_ok.sem, 1)

                    def next_eight(k, s, dst, src):
                        wait_apart(dve, top_ok, top_ok.at(r, first + 2 * k + s - 2))
                        nc.vector.max(dst, src).then_inc(top_ok.sem, 1)

                    for s in range(2):
                        remove(0, s, cut[:, s, 0, :], e8[:, s, :], ex[:, n % 4, s, :])
                    for s in range(2):
                        next_eight(1, s, c8[:, s, 0, :], cut[:, s, 0, :])
                    for s in range(2):
                        remove(2, s, cut[:, s, 1, :], c8[:, s, 0, :], cut[:, s, 0, :])
                    dve.wait_ge(ex_ok.sem, ex_ok.at(r, 2 * n + 1))
                    nc.vector.reciprocal(rden[:, n % 4, :], den[:, n % 2, :]).then_inc(rden_ok.sem, 1)
                    largest(r, n + 1)
                    for s in range(2):
                        next_eight(3, s, c8[:, s, 1, :], cut[:, s, 1, :])
                    for s in range(2):
                        remove(4, s, cut[:, s, 0, :], c8[:, s, 1, :], cut[:, s, 1, :])
                    if n == 2:
                        gelu_lo(r, 1)
                    if n == GROUP + 2:
                        gelu_lo(r, 2)
                    for s in range(2):
                        next_eight(5, s, c8[:, s, 2, :], cut[:, s, 0, :])
                    for s in range(2):
                        remove(6, s, rest[:, n % 2, s, :], c8[:, s, 2, :], cut[:, s, 0, :])

                gelu_lo(0, 0)
                largest(0, 0)
                with dve.Fori(0, R) as r:
                    for n in range(SIDE):
                        step(r, n)

            @block.gpsimd
            def _(pool):
                for s in signals_b["pool"]:
                    s.prime(pool)
                for a in (h2, x1, zz, t_in, rden, zneg, zsc):
                    nc.gpsimd.memset(a[:], 0.0)
                nc.gpsimd.memset(zsq[:], 0.0).then_inc(setup_b["pool"], 1)
                pool.wait_ge(setup_b["dve"], 1)
                for n, op in enumerate((
                        lambda: nc.gpsimd.tensor_scalar(bn_ve[:], bn_mv[:, :, 1], EPS, None, ALU.add),
                        lambda: nc.gpsimd.tensor_tensor(bn_ve[:], bn_ve[:], expo[:, 0:2], ALU.pow),
                        lambda: nc.gpsimd.tensor_tensor(bn_sc[:], bn_ve[:], chan_s[:, :, 1], ALU.mult),
                        lambda: nc.gpsimd.tensor_tensor(bn_bi[:], bn_mv[:, :, 0], bn_sc[:], ALU.mult),
                        lambda: nc.gpsimd.tensor_tensor(bn_bi[:], chan_s[:, :, 2], bn_bi[:], ALU.subtract))):
                    pool.wait_ge(setup_b["pool"], n + 1)
                    op().then_inc(setup_b["pool"], 1)
                pool.wait_ge(setup_b["dve"], 2)

                def step(r, n, tail=False):
                    def due(lag):
                        return not tail or n - lag < 0
                    if due(1):
                        k = n - 1
                        top = TOP_STEPS * (k + 1) - 1
                        slot = k % 2
                        pool.wait_ge(top_ok.sem, top_ok.at(r, top))
                        pool.wait_ge(xs_ok.sem, xs_ok.at(r, k - 2))
                        nc.gpsimd.tensor_tensor(sel[:, slot, IN, :], ex[:, k % 4, IN, :], rest[:, slot, IN, :], ALU.subtract) \
                            .then_inc(sel_ok.sem, 1)
                        pool.wait_ge(sel_ok.sem, sel_ok.at(r, 2 * k))
                        pool.wait_ge(xT_ps.sem, xT_ps.at(r, k - 2))
                        pool.wait_ge(h2_in[k % 4].sem, h2_in[k % 4].at(r, k // 4))
                        nc.gpsimd.tensor_tensor(xs[:, slot, :], sel[:, slot, IN, :], h2[:, k % 4, :], ALU.mult).then_inc(xs_ok.sem, 1)
                        pool.wait_ge(t1_ok.sem, t1_ok.at(r, k - 2))
                        nc.gpsimd.tensor_tensor(sel[:, slot, OUT, :], ex[:, k % 4, OUT, :], rest[:, slot, OUT, :], ALU.subtract) \
                            .then_inc(sel_ok.sem, 1)
                        pool.wait_ge(sel_ok.sem, sel_ok.at(r, 2 * k + 1))
                        pool.wait_ge(tf_ok.sem, tf_ok.at(r, k))
                        nc.gpsimd.tensor_tensor(zz[:, k % 8, :], zz[:, k % 8, :], sel[:, slot, OUT, :], ALU.mult).then_inc(t1_ok.sem, 1)
                    if due(LAG_Z):
                        k = n - LAG_Z
                        z = zz[:, k % 8, :]
                        pool.wait_ge(tin_ok.sem, tin_ok.at(r, k))
                        pool.wait_ge(t1_ok.sem, t1_ok.at(r, k))
                        nc.gpsimd.tensor_tensor(z, z, t_in[:, k % 2, :], ALU.add).then_inc(z0_ok.sem, 1)
                        pool.wait_ge(z0_ok.sem, z0_ok.at(r, k))
                        nc.gpsimd.tensor_tensor(z, z, ffb_b[:], ALU.add).then_inc(z_ok.sem, 1)
                    if due(LAG_NORM):
                        k = n - LAG_NORM
                        wait_apart(pool, zsq_ok, zsq_ok.at(r, k))
                        nc.gpsimd.tensor_scalar(zvar[:], zsq[:, k % 2:k % 2 + 1], 1.0 / D, EPS * FF_SCALE * FF_SCALE, ALU.mult,
                                                ALU.add).then_inc(zvar_ok.sem, 1)
                        pool.wait_ge(zvar_ok.sem, zvar_ok.at(r, k))
                        nc.gpsimd.tensor_tensor(zsc[:, k % 2, 0:1], zvar[:], expo[:, 0:1], ALU.pow).then_inc(zrs_ok.sem, 1)
                        pool.wait_ge(zrs_ok.sem, zrs_ok.at(r, k))
                        nc.gpsimd.tensor_tensor(zsc[:, k % 2, 1:2], zneg[:, k % 4:k % 4 + 1], zsc[:, k % 2, 0:1], ALU.mult) \
                            .then_inc(zsc_ok.sem, 1)
                    if due(LAG_OUT):
                        k = n - LAG_OUT
                        pool.wait_ge(zn_ok.sem, zn_ok.at(r, k))
                        pool.wait_ge(x1_in[k % 4].sem, x1_in[k % 4].at(r, k // 4))
                        nc.gpsimd.tensor_tensor(zn[:, k % 2, :], zn[:, k % 2, :], x1[:, k % 4, :], ALU.add).then_inc(out_ok.sem, 1)

                with pool.Fori(0, R) as r:
                    for n in range(SIDE):
                        step(r, n)
                for n in range(LAG_OUT):
                    step(R, n, tail=True)


OUT_ROWS = B * TILES + 8


def kernel(**inputs):
    import concourse.bacc as bacc
    from concourse.bass_utils import run_bass_kernel_spmd

    def a(name):
        return np.asarray(inputs["L0_" + name])

    def rows(v):
        return np.ascontiguousarray(np.broadcast_to(v.reshape(1, -1), (P, v.size)))

    def columns(v):
        return v.reshape(-1, P).T

    ident = np.eye(P, dtype=np.float32)
    negid = (-np.eye(P) / W_SCALE).astype(np.float16)
    mask = np.zeros((P, 512), np.float32)
    mask[:, 384:] = np.where(np.arange(P)[None, :] > np.arange(P)[:, None], -NEG / S_SCALE, 0.0)
    arrays = {
        "x": a("attn_x"),
        "wqkvo": np.stack([a("attn_W" + w) for w in "qkvo"]),
        "bqk": np.ascontiguousarray(np.stack([columns(a("attn_b" + w)) for w in "qk"], 1)),
        "bv": rows(a("attn_bv")), "bo": rows(a("attn_bo")),
        "ffw": a("ffn_weight"), "ffb": rows(a("ffn_bias")),
        "linw": np.ascontiguousarray(np.stack([a("ffn_so_lin_w").T, a("ffn_si_lin_w").T], 1)),
        "linb": np.stack([a("ffn_so_lin_b"), a("ffn_si_lin_b")])[None],
        "convw": np.ascontiguousarray(np.stack([rows(a("ffn_so_conv_w").ravel()), rows(a("ffn_si_conv_w").ravel())], 1)),
        "chan": np.ascontiguousarray(np.stack([np.stack([a(f"ffn_{s}_{n}") for n in ("conv_b", "gamma", "beta")], 1)
                                               for s in ("so", "si")], 1)),
        "ident": ident, "negid": negid, "mask": mask,
    }
    nc = bacc.Bacc("TRN2", target_bir_lowering=False, num_devices=1)
    aps = [nc.dram_tensor(n, v.shape, mybir.dt.from_np(v.dtype), kind="ExternalInput").ap() for n, v in arrays.items()]
    out = nc.dram_tensor("out", [OUT_ROWS, P, D], F32, kind="ExternalOutput").ap()
    layer_block(nc, *aps, out)
    r = run_bass_kernel_spmd(nc, [arrays], core_ids=[0])
    return np.asarray(r.results[0]["out"])[:B * TILES].reshape(B, S, D)
```

```python
from contextlib import ExitStack

import numpy as np
import concourse.bass as bass
from concourse import mybir

F32 = mybir.dt.float32
F16 = mybir.dt.float16
ALU = mybir.AluOpType
ACT = mybir.ActivationFunctionType
AX = mybir.AxisListType

P = 128
B, S, D = 4, 2048, 512
G = D // 4
C = D // P
TILES = S // P
GROUP = 4
GROUPS = TILES // GROUP
TOPK = 32
EPS = 1e-5
NEG = 10000.0

W_SCALE = 2.0 ** 8
A_SCALE = 2.0 ** 5
P_SCALE = 2.0 ** 13
QKV_DOWN = A_SCALE / (W_SCALE * W_SCALE)
S_SCALE = 1.0 / (A_SCALE * A_SCALE * float(np.sqrt(np.float32(D))))
Y_DOWN = 1.0 / P_SCALE
O_DOWN = 1.0 / (A_SCALE * W_SCALE)
L_DOWN = 1.0 / (A_SCALE * W_SCALE)
FF_SCALE = W_SCALE * W_SCALE
SIDE = 8


def chunks_of(t):
    return t // GROUP + 1


CHUNKS = sum(chunks_of(t) for t in range(TILES))


def chunk_index(t, j):
    return sum(chunks_of(u) for u in range(t)) + j


class Signal:

    def __init__(self, sem, per_round, late=0, step=1):
        self.sem, self.per, self.late, self.step = sem, per_round, late, step

    def prime(self, eng):
        eng.sem_inc(self.sem, (self.per - self.late) * self.step)

    def at(self, r, i):
        return r * (self.per * self.step) + (self.per + i + 1) * self.step


def layer_block(nc, x, wqkvo, bqk, bv, bo, ffw, ffb, linw, linb, convw, chan, ident, negid, mask, out):
    ctx = ExitStack()
    with ctx:
        def sem(name):
            return ctx.enter_context(nc.semaphore(name))

        def sig(name, per, late=0, step=1):
            return Signal(sem(name), per, late, step)

        x1_d = nc.dram_tensor("x1_scratch", [(B + 1) * TILES + GROUP, P, D], F32, kind="Internal").ap()
        h2_d = nc.dram_tensor("h2_scratch", [(B + 1) * TILES, P, D], F32, kind="Internal").ap()
        xc_d = nc.dram_tensor("xc_scratch", [(B + 1) * TILES, P, 2 * P], F32, kind="Internal").ap()
        x_t = x.rearrange("b (t p) d -> (b t) p d", p=P)

        psum = ctx.enter_context(nc.psum_tensor("psum", [P, 8, 512], F32))
        T_BANK = [psum[:, n, :] for n in (0, 1)]
        M_BANK = [psum[:, n, :] for n in (2, 3, 4, 5)]
        Y_BANK = [psum[:, n, :] for n in (6, 7)]

        def keep(name, shape, dt):
            return ctx.enter_context(nc.sbuf_tensor(name, shape, dt))
        idn = keep("idn", [P, P], F32)
        chan_s = keep("chan_s", [P, 2, 3], F32)
        bn_all = keep("bn_all", [P, (B + 1) * TILES, 2, 6], F32)
        expo = keep("expo", [P, 8], F32)

        with ExitStack() as actx:
            def sa(name, shape, dt):
                return actx.enter_context(nc.sbuf_tensor(name, shape, dt))
            w_hi = sa("w_hi", [P, 4, C, D], F16)
            w_lo = sa("w_lo", [P, 4, C, D], F16)
            qT = sa("qT", [P, 2, C, S], F16)
            kT = sa("kT", [P, 2, C, S], F16)
            v = sa("v", [P, 2, TILES, D], F16)
            work = sa("work", [P, 7168], F32)
            hT = [work[:, 2048 * n:2048 * (n + 1)].bitcast(F16).rearrange("p (h c n) -> p h c n", h=2, c=C)
                  for n in (2, 0)]
            xg = work[:, 2048:4096].rearrange("p (j n) -> p j n", j=GROUP)
            raw = work[:, 6144:7168].rearrange("p (s n) -> p s n", s=2)
            sS = [work[:, 2048 * n:2048 * (n + 1)] for n in range(3)]
            pT = work[:, 6144:7168].bitcast(F16).rearrange("p (s h n) -> p s h n", s=2, h=2)
            yn = sa("yn", [P, D], F32)
            yT = sa("yT", [P, 2, C, P], F16)
            ob = sa("ob", [P, 2, D], F32)
            xr = sa("xr", [P, 4, D], F32)
            hb = sa("hb", [P, 2, D], F32)
            prod = sa("prod", [P, D], F32)
            xcs = sa("xcs", [P, 2, 2 * P], F32)
            xcT = sa("xcT", [P, 2, 2, P], F32)
            bo_b = sa("bo_b", [P, D], F32)
            bv_b = sa("bv_b", [P, D], F32)
            cw_b = sa("cw_b", [P, 2, D], F32)
            mask_s = sa("mask_s", [P, 512], F32)
            bqk_s = sa("bqk_s", [P, 2, C], F32)
            st1 = sa("st1", [P, GROUP, 6], F32)
            mv1 = sa("mv1", [P, 2, GROUP, 2], F32)
            ve1 = sa("ve1", [P, GROUP], F32)
            rs1 = sa("rs1", [P, 2, GROUP], F32)
            pm = sa("pm", [P, 3, 4], F32)
            nm = sa("nm", [P, 3], F32)
            ssum = sa("ssum", [P, 3], F32)
            rcp = sa("rcp", [P, 2], F32)
            st2 = sa("st2", [P, 6], F32)
            mv2 = sa("mv2", [P, 2, 2], F32)
            ve2 = sa("ve2", [P, 1], F32)
            rs2 = sa("rs2", [P, 2, 2], F32)
            st3 = sa("st3", [P, 6], F32)
            mv3 = sa("mv3", [P, 2, 2], F32)
            ve3 = sa("ve3", [P, 1], F32)
            rs3 = sa("rs3", [P, 2, 1], F32)

        with ExitStack() as bctx:
            def sc(name, shape, dt):
                return bctx.enter_context(nc.sbuf_tensor(name, shape, dt))
            fw = sc("fw", [P, 2, C, D], F16)
            lw = sc("lw", [P, 2, 2, D], F16)
            lb = sc("lb", [2, 2, D], F16)
            lb_raw = sc("lb_raw", [2, 2, D], F32)
            lb_hi = sc("lb_hi", [2, 2, D], F16)
            ones = sc("ones", [2, P], F16)
            ffb_b = sc("ffb_b", [P, D], F32)
            nid = sc("nid", [P, P], F16)
            wstage = sc("wstage", [P, C, D], F32)
            lstage = sc("lstage", [P, 2, D], F32)
            bn_mv = sc("bn_mv", [P, 2, 2], F32)
            bn_ve = sc("bn_ve", [P, 2], F32)
            bn_sc = sc("bn_sc", [P, 2], F32)
            bn_bi = sc("bn_bi", [P, 2], F32)
            xcg = sc("xcg", [P, 2, GROUP, 2, P], F32)
            xa = sc("xa", [P, GROUP, 2, P], F32)
            xaT = sc("xaT", [P, 2, 2, GROUP, 2, P], F16)
            h2 = sc("h2", [P, 4, D], F32)
            x1 = sc("x1", [P, 4, D], F32)
            h2T = sc("h2T", [P, 2, 2, C, P], F16)
            xsT = sc("xsT", [P, 2, 2, C, P], F16)
            ex = sc("ex", [P, 4, 2, D], F32)
            cut = sc("cut", [P, 2, 2, D], F32)
            rest = sc("rest", [P, 2, 2, D], F32)
            sel = sc("sel", [P, 2, 2, D], F32)
            xs = sc("xs", [P, 2, D], F32)
            zz = sc("zz", [P, 8, D], F32)
            t_in = sc("t_in", [P, 2, D], F32)
            zn = sc("zn", [P, 2, D], F32)
            junk = sc("junk", [P, D], F32)
            m8 = sc("m8", [P, 2, 8], F32)
            e8 = sc("e8", [P, 2, 8], F32)
            c8 = sc("c8", [P, 2, 3, 8], F32)
            nmx = sc("nmx", [P, 2], F32)
            den = sc("den", [P, 2, 2], F32)
            rden = sc("rden", [P, 4, 2], F32)
            zsum = sc("zsum", [P, 2], F32)
            zneg = sc("zneg", [P, 4], F32)
            zsq = sc("zsq", [P, 2], F32)
            zvar = sc("zvar", [P, 1], F32)
            zsc = sc("zsc", [P, 2, 2], F32)

        def attention_steps(i):
            u, t = i - 2, i - 3
            if i < TILES:
                for j in range(chunks_of(i)):
                    yield ("s", i, j)
            if 0 <= t < TILES:
                yield ("yT", t)
            if 0 <= u < TILES:
                for g in range(chunks_of(u)):
                    if g + 1 < chunks_of(u):
                        yield ("pT", u, g + 1)
                    yield ("pv", u, g)
                    if u == TILES - 1:
                        yield ("hT", g)
            if 0 <= u + 1 < TILES:
                yield ("pT", u + 1, 0)
            if 0 <= t < TILES - 1:
                yield ("o", t)
            if 0 <= i - 7 < TILES - 4:
                yield ("x", i - 7)

        def pe_steps():
            for g in range(GROUPS):
                for c in range(C):
                    yield ("k", g, c)
                for c in range(C):
                    yield ("q", g, c)
                    if g + 1 < GROUPS:
                        yield ("hT", GROUP * (g + 1) + c)
                if g == 0:
                    yield ("o", -1)
                for j in range(GROUP):
                    yield ("v", g, j)
                yield ("x", g - 4)
            for i in range(TILES + 3):
                yield from attention_steps(i)

        def transposes_of(i):
            return [s for s in attention_steps(i) if s[0] in ("hT", "pT", "yT")]

        t_items = [s for s in pe_steps() if s[0] in ("hT", "pT", "yT")]
        m_items = [s for s in pe_steps() if s[0] in ("k", "q", "v", "s", "o", "x")]
        t_place = {s: n for n, s in enumerate(t_items)}
        m_place = {s: n for n, s in enumerate(m_items)}
        T_ITEMS = len(t_items)
        assert T_ITEMS % 2 == 0 and len(m_items) % 4 == 0
        t_tail = t_items[t_place["hT", 0]:]

        def t_at(signal, b, step, back=0):
            early = step[0] == "hT" and step[1] < GROUP
            return signal.at(b, t_place[step] - back - (T_ITEMS if early else 0))

        const_in, bias_in, row_out = sem("const_in"), sem("bias_in"), sem("row_out")
        w_in = [sem(f"w_in_{w}") for w in "qkvo"]
        setup_dve, setup_act, setup_pool = sem("setup_dve"), sem("setup_act"), sem("setup_pool")
        xg_in = [sig(f"xg_in{j}", GROUPS, step=16) for j in range(GROUP)]
        xr_in = [sig(f"xr_in{j}", TILES // 4, step=16) for j in range(4)]
        x1_out = [sig(f"x1_out{j}", TILES // 4, late=int(j == 3), step=16) for j in range(4)]
        h2_out = [sig(f"h2_out{j}", TILES // 2, late=1 + j, step=16) for j in range(2)]
        xc_out = [sig(f"xc_out{j}", TILES // 2, late=2, step=16) for j in range(2)]
        ln_stat = sig("ln_stat", TILES)
        ln_mv = sig("ln_mv", TILES)
        ln_ve = sig("ln_ve", GROUPS)
        ln_rs = sig("ln_rs", GROUPS)
        hn_ok = sig("hn_ok", TILES)
        t_ps = sig("t_ps", T_ITEMS, late=len(t_tail))
        t_hi = sig("t_hi", T_ITEMS, late=len(t_tail))
        t_lo = sig("t_lo", T_ITEMS, late=len(t_tail))
        kq_ps = sig("kq_ps", 2 * TILES)
        kq_ev = sig("kq_ev", 2 * TILES)
        kq_lo = sig("kq_lo", 2 * TILES)
        v_ps = sig("v_ps", TILES)
        v_ev = sig("v_ev", TILES)
        v_hi = sig("v_hi", TILES)
        v_lo = sig("v_lo", TILES)
        s_ps = sig("s_ps", CHUNKS)
        s_ev = sig("s_ev", CHUNKS)
        nm_ok = sig("nm_ok", TILES)
        p_ok = sig("p_ok", TILES)
        rcp_ok = sig("rcp_ok", TILES)
        y_ps = sig("y_ps", TILES)
        yn_ok = sig("yn_ok", TILES)
        o_ps = sig("o_ps", TILES, late=1)
        o_ev = sig("o_ev", TILES, late=1)
        relu_ok = sig("relu_ok", TILES, late=1)
        st2_ok = sig("st2_ok", TILES, late=1)
        mv2_ok = sig("mv2_ok", TILES, late=1)
        ve2_ok = sig("ve2_ok", TILES, late=1)
        rsd2_ok = sig("rsd2_ok", TILES, late=1)
        rs2_ok = sig("rs2_ok", TILES, late=1)
        n_ok = sig("n_ok", TILES, late=1)
        x1_ok = sig("x1_ok", TILES, late=1)
        st3_ok = sig("st3_ok", TILES, late=2)
        mv3_ok = sig("mv3_ok", TILES, late=2)
        ve3_ok = sig("ve3_ok", TILES, late=2)
        rs3_ok = sig("rs3_ok", TILES, late=2)
        h2_ok = sig("h2_ok", TILES, late=3)
        pr_ok = sig("pr_ok", 2 * TILES, late=6)
        xc_ok = sig("xc_ok", 2 * TILES, late=6)
        x_ps = sig("x_ps", TILES, late=4)
        x_ev = sig("x_ev", TILES, late=4)
        bn_ok = sig("bn_ok", TILES, late=5)
        signals_of = {
            "pe": [t_ps, kq_ps, v_ps, s_ps, y_ps, o_ps, x_ps],
            "act": [t_hi, kq_ev, v_hi, p_ok, yn_ok, relu_ok, n_ok, x_ev],
            "dve": [ln_stat, ln_mv, hn_ok, t_lo, kq_lo, v_ev, v_lo, s_ev, nm_ok, rcp_ok, o_ev, st2_ok,
                    mv2_ok, st3_ok, mv3_ok, h2_ok, pr_ok, xc_ok, bn_ok],
            "pool": [ln_ve, ln_rs, ve2_ok, rsd2_ok, rs2_ok, x1_ok, ve3_ok, rs3_ok],
            "sp": xg_in + xr_in + x1_out + h2_out + xc_out,
        }

        def t_bank(step):
            return T_BANK[t_place[step] % 2]

        def m_bank(step):
            return M_BANK[m_place[step] % 4]

        def m_freed(step, b):
            kind, *rest = step
            if kind in ("k", "q"):
                return kq_ev, kq_ev.at(b, 8 * rest[0] + 4 * (kind == "q") + rest[1])
            if kind == "v":
                return v_ev, v_ev.at(b, GROUP * rest[0] + rest[1])
            if kind == "s":
                return s_ev, s_ev.at(b, chunk_index(*rest))
            if kind == "o":
                return o_ev, o_ev.at(b, rest[0])
            return x_ev, x_ev.at(b, rest[0])


        passed = sem("passed")

        def wait_apart(eng, signal, value):
            eng.wait_ge(signal.sem, value)
            eng.sem_inc(passed, 1)

        with nc.Block() as block:
            @block.sync
            def _(sp):
                for s in signals_of["sp"]:
                    s.prime(sp)
                sp.dma_start(idn[:], ident).then_inc(const_in, 16)
                for dst, src in ((bqk_s[:], bqk), (bv_b[:], bv)):
                    sp.dma_start(dst, src).then_inc(bias_in, 16)
                w_stage = v[:].rearrange("p h t n -> p (h t n)").bitcast(F32).rearrange("p (w c n) -> p w c n", w=4, c=C)

                def load_x(b, g):
                    for j in range(GROUP):
                        if g:
                            sp.wait_ge(t_ps.sem, t_at(t_ps, b, ("hT", GROUP * (g - 1) + j)))
                        else:
                            last = max(u for u in range(TILES) if u % 3 == 1)
                            sp.wait_ge(t_ps.sem, t_ps.at(b, t_place["pT", last, chunks_of(last) - 1] - T_ITEMS))
                        row = (b % B) * TILES + (GROUP * g + j)
                        sp.dma_start(xg[:, j, :], x_t[bass.ds(row, 1)].rearrange("o p n -> (o p) n")) \
                            .then_inc(xg_in[j].sem, 16)

                def load_residual(b, t):
                    slot = t % 4
                    sp.wait_ge(x1_out[slot].sem, x1_out[slot].at(b, t // 4 - 1))
                    sp.wait_ge(h2_ok.sem, h2_ok.at(b, t - 4))
                    sp.dma_start(xr[:, slot, :], x_t[bass.ds(b * TILES + t, 1)].rearrange("o p n -> (o p) n")) \
                        .then_inc(xr_in[slot].sem, 16)

                def row(d, b, t):
                    return d[bass.ds(b * TILES + (TILES + t), 1)].rearrange("o p n -> (o p) n")

                def store_x1(b, t):
                    sp.wait_ge(x1_ok.sem, x1_ok.at(b, t))
                    sp.dma_start(row(x1_d, b, t), xr[:, t % 4, :]).then_inc(x1_out[t % 4].sem, 16)

                def store_h2(b, t):
                    sp.wait_ge(h2_ok.sem, h2_ok.at(b, t))
                    sp.dma_start(row(h2_d, b, t), hb[:, t % 2, :]).then_inc(h2_out[t % 2].sem, 16)

                def store_xc(b, t):
                    sp.wait_ge(x_ev.sem, x_ev.at(b, t))
                    sp.dma_start(row(xc_d, b, t), xcT[:, t % 2].rearrange("p r n -> p (r n)")) \
                        .then_inc(xc_out[t % 2].sem, 16)

                def late_stores(b, g):
                    if g == 0:
                        store_x1(b, -1)
                    if g < 3:
                        store_h2(b, g - 3)

                load_x(0, 0)
                for w in (1, 0, 2, 3):
                    sp.dma_start(w_stage[:, w], wqkvo[w].rearrange("(c p) n -> p c n", p=P)).then_inc(w_in[w], 16)
                load_x(0, 1)
                for dst, src in ((chan_s[:], chan), (bo_b[:], bo), (cw_b[:], convw), (mask_s[:], mask)):
                    sp.dma_start(dst, src).then_inc(const_in, 16)
                sp.wait_ge(setup_pool, 2)
                sp.dma_start(h2_d[TILES - GROUP], hb[:, 0, :]).then_inc(row_out, 16)
                for n in (2, 3):
                    sp.dma_start(x1_d[(B + 1) * TILES + n], hb[:, 0, :]).then_inc(row_out, 16)
                sp.wait_ge(row_out, 16 * 3)

                with sp.Fori(0, B) as b:
                    for g in range(GROUPS):
                        late_stores(b, g)
                        if g + 2 < GROUPS:
                            load_x(b, g + 2)
                        store_xc(b, g - 4)
                    for i in range(TILES + 3):
                        if i == TILES - 1:
                            load_x(b + 1, 0)
                        if i == TILES + 1:
                            load_x(b + 1, 1)
                        if 0 <= i - 2 < TILES:
                            load_residual(b, i - 2)
                        if 0 <= i - 4 < TILES:
                            store_x1(b, i - 4)
                        if 0 <= i - 6 < TILES:
                            store_h2(b, i - 6)
                        if 0 <= i - 7 < TILES - 4:
                            store_xc(b, i - 7)
                for g in range(GROUPS):
                    late_stores(B, g)
                    store_xc(B, g - 4)
                for s in xg_in:
                    sp.wait_ge(s.sem, s.at(B, 1))
                for s in x1_out + h2_out + xc_out:
                    sp.wait_ge(s.sem, s.at(B, -1))

            @block.tensor
            def _(pe):
                for s in signals_of["pe"]:
                    s.prime(pe)
                pe.wait_ge(const_in, 16)

                def three(outp, n, total, stat, mov):
                    for k, (a, c) in enumerate(((0, 0), (0, 1), (1, 0))):
                        mm = nc.tensor.matmul(outp, stat(a), mov(c), start=(n == 0 and k == 0),
                                              stop=(n == total - 1 and k == 2))
                    return mm

                def take_t(b, step):
                    pe.wait_ge(t_lo.sem, t_at(t_lo, b, step, 2))
                    return t_bank(step)

                def take_m(b, step):
                    n = m_place[step]
                    before = m_items[n - 4]
                    signal, value = m_freed(before, b if n >= 4 else b - 1)
                    pe.wait_ge(signal.sem, value)
                    return m_bank(step)

                def output_projection(b, t, bank):
                    last = t_place["yT", t % TILES] - (T_ITEMS if t < 0 else 0)
                    pe.wait_ge(t_lo.sem, t_lo.at(b, last))
                    for n in range(C):
                        mm = three(bank, n, C, lambda a: yT[:, a, n, :], lambda a: (w_hi, w_lo)[a][:, 3, n, :])
                    mm.then_inc(o_ps.sem, 1)

                def conv_transposes(b, t, bank):
                    pe.wait_ge(xc_ok.sem, xc_ok.at(b, 2 * t + 1))
                    for r in range(2):
                        mm = nc.tensor.transpose(bank[:, P * r:P * (r + 1)], xcs[:, t % 2, P * r:P * (r + 1)], idn[:])
                    mm.then_inc(x_ps.sem, 1)

                def transpose_h(b, step):
                    t, bank = step[1], take_t(b, step)
                    pe.wait_ge(hn_ok.sem, hn_ok.at(b, t))
                    for c in range(C):
                        mm = nc.tensor.transpose(bank[:, P * c:P * (c + 1)], xg[:, t % GROUP, P * c:P * (c + 1)], idn[:])
                    mm.then_inc(t_ps.sem, 1)

                for step in t_tail:
                    if step[0] == "hT":
                        transpose_h(0, step)
                    else:
                        pe.wait_ge(t_ps.sem, t_place[step])
                        pe.sem_inc(t_ps.sem, 1)
                pe.wait_ge(setup_pool, 2)
                with pe.Fori(0, B) as b:
                    for step in pe_steps():
                        kind, *at = step
                        if kind == "hT":
                            transpose_h(b + 1 if at[0] < GROUP else b, step)
                        elif kind in ("k", "q"):
                            g, c = at
                            bank = take_m(b, step)
                            if kind == "k" and c == 0:
                                pe.wait_ge(t_lo.sem, t_at(t_lo, b, ("hT", GROUP * g + GROUP - 1)))
                            if g == 0 and c == 0:
                                pe.wait_ge(setup_dve, 1 if kind == "k" else 2)
                            w, h = (1 if kind == "k" else 0), hT[g % 2]
                            for n in range(C):
                                mm = three(bank, n, C, lambda a: (w_hi, w_lo)[a][:, w, n, P * c:P * (c + 1)], lambda a: h[:, a, n, :])
                            mm.then_inc(kq_ps.sem, 1)
                        elif kind == "v":
                            g, j = at
                            bank, h = take_m(b, step), hT[g % 2]
                            if g == 0 and j == 0:
                                pe.wait_ge(setup_dve, 3)
                            for n in range(C):
                                mm = three(bank, n, C, lambda a: h[:, a, n, P * j:P * (j + 1)], lambda a: (w_hi, w_lo)[a][:, 2, n, :])
                            mm.then_inc(v_ps.sem, 1)
                        elif kind == "s":
                            t, j = at
                            bank = take_m(b, step)
                            if t == 0:
                                pe.wait_ge(kq_lo.sem, kq_lo.at(b, 2 * TILES - 1))
                            w = min(512, P * (t + 1) - 512 * j)
                            for n in range(C):
                                mm = three(bank[:, 0:w], n, C, lambda a: qT[:, a, n, P * t:P * (t + 1)],
                                           lambda a: kT[:, a, n, 512 * j:512 * j + w])
                            mm.then_inc(s_ps.sem, 1)
                        elif kind == "pT":
                            u, g = at
                            bank = take_t(b, step)
                            pe.wait_ge(p_ok.sem, p_ok.at(b, u))
                            for n in range(min(GROUP, u + 1 - GROUP * g)):
                                k = 512 * g + P * n
                                mm = nc.tensor.transpose(bank[:, P * n:P * (n + 1)], sS[u % 3][:, k:k + P], idn[:])
                            mm.then_inc(t_ps.sem, 1)
                        elif kind == "pv":
                            u, g = at
                            if u == 0:
                                pe.wait_ge(v_lo.sem, v_lo.at(b, TILES - 1))
                            if g == 0:
                                pe.wait_ge(yn_ok.sem, yn_ok.at(b, u - 2))
                            pe.wait_ge(t_lo.sem, t_lo.at(b, t_place["pT", u, g]))
                            slot = chunk_index(u, g) % 2
                            for n in range(min(GROUP, u + 1 - GROUP * g)):
                                mm = three(Y_BANK[u % 2], GROUP * g + n, u + 1, lambda a: pT[:, slot, a, P * n:P * (n + 1)],
                                           lambda a: v[:, a, GROUP * g + n, :])
                            if g == chunks_of(u) - 1:
                                mm.then_inc(y_ps.sem, 1)
                        elif kind == "yT":
                            t, = at
                            bank = take_t(b, step)
                            pe.wait_ge(yn_ok.sem, yn_ok.at(b, t))
                            for c in range(C):
                                mm = nc.tensor.transpose(bank[:, P * c:P * (c + 1)], yn[:, P * c:P * (c + 1)], idn[:])
                            mm.then_inc(t_ps.sem, 1)
                        elif kind == "o":
                            if at[0] < 0:
                                pe.wait_ge(setup_dve, 4)
                            output_projection(b, at[0], take_m(b, step))
                        else:
                            t, = at
                            conv_transposes(b, t, take_m(b, step))
                pe.wait_ge(s_ev.sem, s_ev.at(B, -1))
                pe.wait_ge(o_ev.sem, o_ev.at(B, -2))
                pe.wait_ge(x_ev.sem, x_ev.at(B, -5))
                output_projection(B, -1, m_bank(("o", -1)))
                for g in range(GROUPS):
                    pe.wait_ge(x_ev.sem, x_ev.at(B, g - 5))
                    conv_transposes(B, g - 4, m_bank(("x", g - 4)))

            @block.scalar
            def _(act):
                for s in signals_of["act"]:
                    s.prime(act)
                w_stage = v[:].rearrange("p h t n -> p (h t n)").bitcast(F32).rearrange("p (w c n) -> p w c n", w=4, c=C)

                def weight_hi(w):
                    act.wait_ge(w_in[w], 16)
                    nc.scalar.activation(w_hi[:, w], w_stage[:, w], ACT.Copy, scale=W_SCALE).then_inc(setup_act, 1)

                def hi_half(b, step, dst, scale):
                    act.wait_ge(t_ps.sem, t_at(t_ps, b, step))
                    src = t_bank(step)[:, 0:dst.shape[-1]] if len(dst.shape) == 2 else t_bank(step).rearrange("p (c n) -> p c n", c=C)
                    nc.scalar.activation(dst, src, ACT.Copy, scale=scale).then_inc(t_hi.sem, 1)

                def hi_h(b, t):
                    j = t % GROUP
                    hi_half(b, ("hT", t), hT[(t // GROUP) % 2][:, 0, :, P * j:P * (j + 1)], W_SCALE)

                def relu_kq(b, g, kind, c):
                    n = 8 * g + 4 * kind + c
                    step = ("kq"[kind], g, c)
                    act.wait_ge(kq_ps.sem, kq_ps.at(b, n))
                    act.wait_ge(kq_lo.sem, kq_lo.at(b, n - 2))
                    if kind == 0 and c < 2:
                        act.wait_ge(v_lo.sem, v_lo.at(b, GROUP * g - 1))
                    dst, bias = (kT, qT)[kind], bqk_s[:, 1 - kind, c:c + 1]
                    nc.scalar.activation(raw[:, n % 2, :], m_bank(step), ACT.Relu, bias=bias, scale=QKV_DOWN)
                    nc.scalar.activation(dst[:, 0, c, 512 * g:512 * (g + 1)], m_bank(step), ACT.Relu, bias=bias,
                                         scale=QKV_DOWN).then_inc(kq_ev.sem, 1)

                def hi_v(b, t):
                    act.wait_ge(v_ev.sem, v_ev.at(b, t))
                    nc.scalar.activation(v[:, 0, t, :], raw[:, t % 2, :], ACT.Relu).then_inc(v_hi.sem, 1)

                def relu_o(b, t):
                    act.wait_ge(o_ev.sem, o_ev.at(b, t))
                    nc.scalar.activation(ob[:, t % 2, :], ob[:, t % 2, :], ACT.Relu).then_inc(relu_ok.sem, 1)

                def normed(b, t):
                    act.wait_ge(rs2_ok.sem, rs2_ok.at(b, t))
                    nc.scalar.activation(ob[:, t % 2, :], ob[:, t % 2, :], ACT.Identity, bias=rs2[:, t % 2, 1:2],
                                         scale=rs2[:, t % 2, 0:1]).then_inc(n_ok.sem, 1)

                def conv_out(b, t):
                    act.wait_ge(x_ps.sem, x_ps.at(b, t))
                    act.wait_ge(xc_out[t % 2].sem, xc_out[t % 2].at(b, t // 2 - 1))
                    act.wait_ge(bn_ok.sem, bn_ok.at(b, t - 2))
                    for r in range(2):
                        i = nc.scalar.activation(xcT[:, t % 2, r, :], m_bank(("x", t if t < 12 else t - 16))[:, P * r:P * (r + 1)],
                                                 ACT.Identity, bias=chan_s[:, r, 0:1])
                    i.then_inc(x_ev.sem, 1)

                def hi_of(b, step):
                    kind, *at = step
                    if kind == "hT":
                        hi_h(b + 1 if at[0] < GROUP else b, at[0])
                    elif kind == "yT":
                        hi_half(b, step, yT[:, 0], Y_DOWN)
                    else:
                        u, g = at
                        hi_half(b, step, pT[:, chunk_index(u, g) % 2, 0, 0:P * min(GROUP, u + 1 - GROUP * g)], P_SCALE)

                weight_hi(1)
                for step in t_tail:
                    if step[0] == "hT":
                        hi_h(0, step[1])
                    else:
                        act.wait_ge(t_hi.sem, t_place[step])
                        act.sem_inc(t_hi.sem, 1)
                weight_hi(0)
                weight_hi(2)
                weight_hi(3)
                act.wait_ge(setup_dve, 1)
                act.wait_ge(const_in, 16 * 5)
                act.wait_ge(setup_pool, 2)
                with act.Fori(0, B) as b:
                    for g in range(GROUPS):
                        for c in range(C):
                            relu_kq(b, g, 0, c)
                        for c in range(C):
                            relu_kq(b, g, 1, c)
                            if g + 1 < GROUPS:
                                hi_of(b, ("hT", GROUP * (g + 1) + c))
                        if g == 0:
                            relu_o(b, -1)
                            normed(b, -1)
                        for j in range(GROUP):
                            hi_v(b, GROUP * g + j)
                        conv_out(b, g - 4)
                    for i in range(TILES + 3):
                        u, t = i - 2, i - 3
                        for step in transposes_of(i):
                            hi_of(b, step)
                        if i < TILES:
                            w = P * (i + 1)
                            act.wait_ge(nm_ok.sem, nm_ok.at(b, i))
                            nc.scalar.activation(sS[i % 3][:, 0:w], sS[i % 3][:, 0:w], ACT.Exp, bias=nm[:, i % 3:i % 3 + 1],
                                                 accum_out=ssum[:, i % 3:i % 3 + 1]).then_inc(p_ok.sem, 1)
                        if 0 <= u < TILES:
                            act.wait_ge(y_ps.sem, y_ps.at(b, u))
                            act.wait_ge(rcp_ok.sem, rcp_ok.at(b, u))
                            nc.scalar.activation(yn[:], Y_BANK[u % 2], ACT.Copy, scale=rcp[:, u % 2:u % 2 + 1]) \
                                .then_inc(yn_ok.sem, 1)
                        if 0 <= t < TILES - 1:
                            relu_o(b, t)
                        if 0 <= i - 4 < TILES:
                            normed(b, i - 4)
                        if 0 <= i - 7 < TILES - 4:
                            conv_out(b, i - 7)
                relu_o(B, -1)
                normed(B, -1)
                for g in range(GROUPS):
                    conv_out(B, g - 4)

            @block.vector
            def _(dve):
                for s in signals_of["dve"]:
                    s.prime(dve)
                w_stage = v[:].rearrange("p h t n -> p (h t n)").bitcast(F32).rearrange("p (w c n) -> p w c n", w=4, c=C)
                def weight_lo(n, w):
                    dve.wait_ge(setup_act, n + 1)
                    nc.vector.scalar_tensor_tensor(w_lo[:, w], w_stage[:, w], W_SCALE, w_hi[:, w], ALU.mult, ALU.subtract) \
                        .then_inc(setup_dve, 1)

                def lo_half(b, step, dst, hi, scale):
                    dve.wait_ge(t_hi.sem, t_at(t_hi, b, step))
                    src = t_bank(step)[:, 0:dst.shape[-1]] if len(dst.shape) == 2 else t_bank(step).rearrange("p (c n) -> p c n", c=C)
                    nc.vector.scalar_tensor_tensor(dst, src, scale, hi, ALU.mult, ALU.subtract).then_inc(t_lo.sem, 1)

                def lo_h(b, t):
                    j, h = t % GROUP, hT[(t // GROUP) % 2]
                    lo_half(b, ("hT", t), h[:, 1, :, P * j:P * (j + 1)], h[:, 0, :, P * j:P * (j + 1)], W_SCALE)

                def ln_stats(b, g, j):
                    dve.wait_ge(xg_in[j].sem, xg_in[j].at(b, g))
                    nc.vector.bn_stats(st1[:, j, :], xg[:, j, :]).then_inc(ln_stat.sem, 1)
                    wait_apart(dve, ln_stat, ln_stat.at(b, GROUP * g + j))
                    nc.vector.bn_aggr(mv1[:, g % 2, j, :], st1[:, j, :]).then_inc(ln_mv.sem, 1)

                def ln_norm(b, g):
                    dve.wait_ge(ln_rs.sem, ln_rs.at(b, g))
                    for j in range(GROUP):
                        nc.vector.tensor_scalar(xg[:, j, :], xg[:, j, :], mv1[:, g % 2, j, 0:1], rs1[:, g % 2, j:j + 1],
                                                ALU.subtract, ALU.mult).then_inc(hn_ok.sem, 1)

                def lo_kq(b, g, kind, c):
                    n = 8 * g + 4 * kind + c
                    dst = (kT, qT)[kind][:, :, c, 512 * g:512 * (g + 1)]
                    dve.wait_ge(kq_ev.sem, kq_ev.at(b, n))
                    nc.vector.tensor_tensor(dst[:, 1], raw[:, n % 2, :], dst[:, 0], ALU.subtract).then_inc(kq_lo.sem, 1)

                def bias_v(b, g, j):
                    t = GROUP * g + j
                    dve.wait_ge(v_ps.sem, v_ps.at(b, t))
                    if j < 2:
                        dve.wait_ge(kq_lo.sem, kq_lo.at(b, 8 * g + 7))
                    else:
                        dve.wait_ge(v_lo.sem, v_lo.at(b, t - 2))
                    nc.vector.scalar_tensor_tensor(raw[:, t % 2, :], m_bank(("v", g, j)), QKV_DOWN, bv_b[:], ALU.mult, ALU.add) \
                        .then_inc(v_ev.sem, 1)

                def lo_v(b, t):
                    dve.wait_ge(v_hi.sem, v_hi.at(b, t))
                    nc.vector.scalar_tensor_tensor(v[:, 1, t, :], raw[:, t % 2, :], 0.0, v[:, 0, t, :], ALU.max, ALU.subtract) \
                        .then_inc(v_lo.sem, 1)

                def bias_o(b, t):
                    dve.wait_ge(o_ps.sem, o_ps.at(b, t))
                    dve.wait_ge(x1_ok.sem, x1_ok.at(b, t - 2))
                    nc.vector.scalar_tensor_tensor(ob[:, t % 2, :], m_bank(("o", t)), O_DOWN, bo_b[:], ALU.mult, ALU.add) \
                        .then_inc(o_ev.sem, 1)

                def attention_stats(b, t):
                    dve.wait_ge(relu_ok.sem, relu_ok.at(b, t))
                    nc.vector.bn_stats(st2[:], ob[:, t % 2, :]).then_inc(st2_ok.sem, 1)
                    wait_apart(dve, st2_ok, st2_ok.at(b, t))
                    nc.vector.bn_aggr(mv2[:, t % 2, :], st2[:]).then_inc(mv2_ok.sem, 1)

                def residual_stats(b, t):
                    dve.wait_ge(x1_ok.sem, x1_ok.at(b, t))
                    nc.vector.bn_stats(st3[:], xr[:, t % 4, :]).then_inc(st3_ok.sem, 1)
                    wait_apart(dve, st3_ok, st3_ok.at(b, t))
                    nc.vector.bn_aggr(mv3[:, t % 2, :], st3[:]).then_inc(mv3_ok.sem, 1)

                def second_norm(b, t):
                    dve.wait_ge(rs3_ok.sem, rs3_ok.at(b, t))
                    dve.wait_ge(h2_out[t % 2].sem, h2_out[t % 2].at(b, t // 2 - 1))
                    dve.wait_ge(xc_ok.sem, xc_ok.at(b, 2 * t - 3))
                    nc.vector.tensor_scalar(hb[:, t % 2, :], xr[:, t % 4, :], mv3[:, t % 2, 0:1], rs3[:, t % 2, 0:1],
                                            ALU.subtract, ALU.mult).then_inc(h2_ok.sem, 1)

                def convolution(b, t, r):
                    dve.wait_ge(h2_ok.sem, h2_ok.at(b, t))
                    dve.wait_ge(xc_ok.sem, xc_ok.at(b, 2 * t + r - 1))
                    nc.vector.tensor_tensor(prod[:], hb[:, t % 2, :], cw_b[:, r, :], ALU.mult).then_inc(pr_ok.sem, 1)
                    dve.wait_ge(pr_ok.sem, pr_ok.at(b, 2 * t + r))
                    dve.wait_ge(x_ps.sem, x_ps.at(b, t - 2))
                    nc.vector.tensor_reduce(xcs[:, t % 2, P * r:P * (r + 1)], prod[:].rearrange("p (g f) -> p g f", f=4),
                                            AX.X, ALU.add).then_inc(xc_ok.sem, 1)

                def conv_stats(b, t):
                    for r in range(2):
                        wait_apart(dve, x_ev, x_ev.at(b, t))
                        i = nc.vector.bn_stats(bn_all[:, bass.ds(b * TILES + (TILES + t), 1), r, :].rearrange("p o s -> p (o s)"),
                                               xcT[:, t % 2, r, :])
                    i.then_inc(bn_ok.sem, 1)

                def late_tiles(b, g):
                    if g == 0:
                        bias_o(b, -1)
                    if g < 3:
                        second_norm(b, g - 3)
                    if g == 0:
                        attention_stats(b, -1)
                    if g < 3:
                        for r in range(2):
                            convolution(b, g - 3, r)
                    if g < 2:
                        residual_stats(b, g - 2)
                    conv_stats(b, g - 5)

                def lo_of(b, step):
                    kind, *at = step
                    if kind == "hT":
                        lo_h(b + 1 if at[0] < GROUP else b, at[0])
                    elif kind == "yT":
                        lo_half(b, step, yT[:, 1], yT[:, 0], Y_DOWN)
                    else:
                        u, g = at
                        d = pT[:, chunk_index(u, g) % 2, :, 0:P * min(GROUP, u + 1 - GROUP * g)]
                        lo_half(b, step, d[:, 1], d[:, 0], P_SCALE)

                for j in range(GROUP):
                    ln_stats(0, 0, j)
                ln_norm(0, 0)
                dve.wait_ge(bias_in, 16 * 2)
                nc.vector.tensor_scalar(bqk_s[:], bqk_s[:], A_SCALE, None, ALU.mult)
                nc.vector.tensor_scalar(bv_b[:], bv_b[:], A_SCALE, None, ALU.mult)
                for step in t_tail:
                    if step[0] == "hT":
                        lo_h(0, step[1])
                    else:
                        dve.wait_ge(t_lo.sem, t_place[step])
                        dve.sem_inc(t_lo.sem, 1)
                weight_lo(0, 1)
                weight_lo(1, 0)
                weight_lo(2, 2)
                weight_lo(3, 3)
                dve.wait_ge(setup_dve, 4)
                dve.wait_ge(const_in, 16 * 5)
                dve.wait_ge(setup_pool, 2)
                with dve.Fori(0, B) as b:
                    for g in range(GROUPS):
                        if g + 1 < GROUPS:
                            for j in range(GROUP):
                                ln_stats(b, g + 1, j)
                        for c in range(C):
                            lo_kq(b, g, 0, c)
                            if c == 1 and g + 1 < GROUPS:
                                ln_norm(b, g + 1)
                        for c in range(C):
                            lo_kq(b, g, 1, c)
                            if g + 1 < GROUPS:
                                lo_of(b, ("hT", GROUP * (g + 1) + c))
                        late_tiles(b, g)
                        bias_v(b, g, 0)
                        for j in range(1, GROUP):
                            bias_v(b, g, j)
                            lo_v(b, GROUP * g + j - 1)
                        lo_v(b, GROUP * g + GROUP - 1)
                    conv_stats(b, -1)
                    for i in range(TILES + 3):
                        u, t = i - 2, i - 3
                        if 0 <= i - 4 < TILES and i < TILES:
                            attention_stats(b, i - 4)
                        if i < TILES:
                            slot = i % 3
                            for j in range(chunks_of(i)):
                                w, n = min(512, P * (i + 1) - 512 * j), chunk_index(i, j)
                                src, dst = m_bank(("s", i, j))[:, 0:w], sS[slot][:, 512 * j:512 * j + w]
                                wait_apart(dve, s_ps, s_ps.at(b, n))
                                if j + 1 < chunks_of(i):
                                    nc.vector.tensor_scalar(dst, src, S_SCALE, None, ALU.mult, ALU.max,
                                                            accum_out=pm[:, slot, j:j + 1]).then_inc(s_ev.sem, 1)
                                else:
                                    nc.vector.tensor_tensor_reduce(out=dst, in0=src, in1=mask_s[:, 512 - w:512], scale=S_SCALE,
                                                                   scalar=-3e38, op0=ALU.add, op1=ALU.max,
                                                                   accum_out=pm[:, slot, j:j + 1]).then_inc(s_ev.sem, 1)
                            dve.wait_ge(s_ev.sem, s_ev.at(b, chunk_index(i, chunks_of(i) - 1)))
                            nc.vector.tensor_reduce(nm[:, slot:slot + 1], pm[:, slot, 0:chunks_of(i)], AX.X, ALU.max,
                                                    negate=True).then_inc(nm_ok.sem, 1)
                        between = []
                        if 0 <= i - 6 < TILES:
                            between += [lambda: second_norm(b, i - 6), lambda: convolution(b, i - 6, 0),
                                        lambda: convolution(b, i - 6, 1)]
                        if 0 <= i - 5 < TILES:
                            between.append(lambda: residual_stats(b, i - 5))
                        if 0 <= i - 4 < TILES and i >= TILES:
                            between.insert(0, lambda: attention_stats(b, i - 4))
                        if i == TILES:
                            between[1:1] = [lambda j=j: ln_stats(b + 1, 0, j) for j in range(GROUP)]
                            between.insert(-2, lambda: ln_norm(b + 1, 0))
                        halves = transposes_of(i)
                        for n, step in enumerate(halves):
                            lo_of(b, step)
                            if n == 0 and 0 <= u < TILES:
                                dve.wait_ge(p_ok.sem, p_ok.at(b, u))
                                nc.vector.reciprocal(rcp[:, u % 2:u % 2 + 1], ssum[:, u % 3:u % 3 + 1]).then_inc(rcp_ok.sem, 1)
                            if n:
                                for _ in range(-(-len(between) // (len(halves) - n))):
                                    between.pop(0)()
                        for later in between:
                            later()
                        if 0 <= t < TILES - 1:
                            bias_o(b, t)
                        if 0 <= i - 8 < TILES:
                            conv_stats(b, i - 8)
                for g in range(GROUPS):
                    late_tiles(B, g)
                conv_stats(B, -1)
                dve.wait_ge(bn_ok.sem, bn_ok.at(B, -1))

            @block.gpsimd
            def _(pool):
                for s in signals_of["pool"]:
                    s.prime(pool)
                nc.gpsimd.memset(expo[:], -0.5).then_inc(setup_pool, 1)

                def ln_scale(b, g):
                    wait_apart(pool, ln_mv, ln_mv.at(b, GROUP * g + GROUP - 1))
                    nc.gpsimd.tensor_scalar(ve1[:], mv1[:, g % 2, :, 1], EPS, None, ALU.add).then_inc(ln_ve.sem, 1)
                    pool.wait_ge(ln_ve.sem, ln_ve.at(b, g))
                    nc.gpsimd.tensor_tensor(rs1[:, g % 2, :], ve1[:], expo[:, 0:GROUP], ALU.pow).then_inc(ln_rs.sem, 1)

                def attention_scale(b, t):
                    m = mv2[:, t % 2, :]
                    wait_apart(pool, mv2_ok, mv2_ok.at(b, t))
                    nc.gpsimd.tensor_scalar(ve2[:], m[:, 1:2], EPS, None, ALU.add).then_inc(ve2_ok.sem, 1)
                    pool.wait_ge(ve2_ok.sem, ve2_ok.at(b, t))
                    nc.gpsimd.tensor_tensor(rs2[:, t % 2, 0:1], ve2[:], expo[:, 0:1], ALU.pow).then_inc(rsd2_ok.sem, 1)
                    wait_apart(pool, rsd2_ok, rsd2_ok.at(b, t))
                    nc.gpsimd.tensor_scalar(rs2[:, t % 2, 1:2], m[:, 0:1], rs2[:, t % 2, 0:1], -1.0, ALU.mult, ALU.mult) \
                        .then_inc(rs2_ok.sem, 1)

                def residual(b, t):
                    pool.wait_ge(n_ok.sem, n_ok.at(b, t))
                    pool.wait_ge(xr_in[t % 4].sem, xr_in[t % 4].at(b, t // 4))
                    nc.gpsimd.tensor_tensor(xr[:, t % 4, :], ob[:, t % 2, :], xr[:, t % 4, :], ALU.add).then_inc(x1_ok.sem, 1)

                def second_scale(b, t):
                    wait_apart(pool, mv3_ok, mv3_ok.at(b, t))
                    nc.gpsimd.tensor_scalar(ve3[:], mv3[:, t % 2, 1:2], EPS, None, ALU.add).then_inc(ve3_ok.sem, 1)
                    pool.wait_ge(ve3_ok.sem, ve3_ok.at(b, t))
                    nc.gpsimd.tensor_tensor(rs3[:, t % 2, :], ve3[:], expo[:, 0:1], ALU.pow).then_inc(rs3_ok.sem, 1)

                def late_tiles(b, g):
                    if g == 0:
                        attention_scale(b, -1)
                    if g < 2:
                        second_scale(b, g - 2)
                    if g == 0:
                        residual(b, -1)

                pool.wait_ge(setup_pool, 1)
                ln_scale(0, 0)
                for a in (yT, ob, xr, hb, xcs, xcT, mv2, mv3, rs2, rs3):
                    nc.gpsimd.memset(a[:], 0.0)
                nc.gpsimd.memset(bn_all[:], 0.0).then_inc(setup_pool, 1)
                pool.wait_ge(setup_pool, 2)
                with pool.Fori(0, B) as b:
                    for g in range(GROUPS):
                        if g + 1 < GROUPS:
                            ln_scale(b, g + 1)
                        late_tiles(b, g)
                    for i in range(TILES + 3):
                        if 0 <= i - 4 < TILES:
                            attention_scale(b, i - 4)
                        if i == TILES:
                            ln_scale(b + 1, 0)
                        if 0 <= i - 5 < TILES:
                            second_scale(b, i - 5)
                        if 0 <= i - 4 < TILES:
                            residual(b, i - 4)
                for g in range(GROUPS):
                    late_tiles(B, g)

        R = B * TILES // SIDE

        def sig_b(name, per, late=0, step=1):
            return Signal(sem("b_" + name), per, late, step)

        LAG_IN, LAG_Z, LAG_STAT, LAG_NORM, LAG_OUT = 2, 3, 4, 5, 6
        TOP_STEPS = 2 * (2 * (TOPK // 8) - 1)
        setup_b = {e: sem("setup_b_" + e) for e in ("lin", "ffw", "act", "dve", "pool")}
        xc_in = [sig_b(f"xc_in{n}", 1, step=16) for n in range(2)]
        h2_in = [sig_b(f"h2_in{n}", SIDE // 4, step=16) for n in range(4)]
        x1_in = [sig_b(f"x1_in{n}", SIDE // 4, late=int(n >= 2), step=16) for n in range(4)]
        out_st = [sig_b(f"out_st{n}", SIDE // 2, late=LAG_OUT // 2, step=16) for n in range(2)]
        gelu_ok = sig_b("gelu_ok", 2)
        xa_hi = sig_b("xa_hi", 2)
        xa_lo = sig_b("xa_lo", 2)
        lg_ps = sig_b("lg_ps", 2 * SIDE)
        mx_ok = sig_b("mx_ok", 2 * SIDE)
        nmx_ok = sig_b("nmx_ok", 2 * SIDE)
        e8_ok = sig_b("e8_ok", 2 * SIDE)
        ex_ok = sig_b("ex_ok", 2 * SIDE)
        top_ok = sig_b("top_ok", TOP_STEPS * SIDE)
        rden_ok = sig_b("rden_ok", SIDE)
        sel_ok = sig_b("sel_ok", 2 * SIDE, late=2)
        xs_ok = sig_b("xs_ok", SIDE, late=1)
        hT_ps = sig_b("hT_ps", SIDE)
        hT_hi = sig_b("hT_hi", SIDE)
        hm_ps = sig_b("hm_ps", SIDE)
        hT_lo = sig_b("hT_lo", SIDE)
        xT_ps = sig_b("xT_ps", SIDE, late=1)
        xT_hi = sig_b("xT_hi", SIDE, late=1)
        xm_ps = sig_b("xm_ps", SIDE, late=1)
        xT_lo = sig_b("xT_lo", SIDE, late=1)
        full_ps = sig_b("full_ps", SIDE, late=1)
        tf_ok = sig_b("tf_ok", SIDE, late=1)
        t1_ok = sig_b("t1_ok", SIDE, late=1)
        in_ps = sig_b("in_ps", SIDE, late=LAG_IN)
        tin_ok = sig_b("tin_ok", SIDE, late=LAG_IN)
        z0_ok = sig_b("z0_ok", SIDE, late=LAG_Z)
        z_ok = sig_b("z_ok", SIDE, late=LAG_Z)
        zsum_ok = sig_b("zsum_ok", SIDE, late=LAG_STAT)
        zneg_ok = sig_b("zneg_ok", SIDE, late=LAG_STAT)
        zsq_ok = sig_b("zsq_ok", SIDE, late=LAG_STAT)
        zvar_ok = sig_b("zvar_ok", SIDE, late=LAG_NORM)
        zrs_ok = sig_b("zrs_ok", SIDE, late=LAG_NORM)
        zsc_ok = sig_b("zsc_ok", SIDE, late=LAG_NORM)
        zn_ok = sig_b("zn_ok", SIDE, late=LAG_NORM)
        out_ok = sig_b("out_ok", SIDE, late=LAG_OUT)
        signals_b = {
            "sp": xc_in + h2_in + x1_in + out_st,
            "pe": [lg_ps, hT_ps, hm_ps, xT_ps, xm_ps, full_ps, in_ps],
            "act": [gelu_ok, xa_hi, nmx_ok, e8_ok, ex_ok, hT_hi, hT_lo, xT_hi, xT_lo, tf_ok, tin_ok, zsum_ok,
                    zneg_ok, zsq_ok, zn_ok],
            "dve": [xa_lo, mx_ok, top_ok, rden_ok],
            "pool": [sel_ok, xs_ok, t1_ok, z0_ok, z_ok, zvar_ok, zrs_ok, zsc_ok, out_ok],
        }
        L_BANK = [psum[:, n, :] for n in (0, 1)]
        HT_BANK, XT_BANK = psum[:, 2, :], psum[:, 3, :]
        F_BANK = [psum[:, n, :] for n in (4, 5)]
        I_BANK = [psum[:, n, :] for n in (6, 7)]
        OUT, IN = 0, 1

        def tile_row(r, n):
            return r * -SIDE + (B * TILES - GROUP - GROUP * (n // GROUP) + n % GROUP)

        with nc.Block() as block:
            @block.sync
            def _(sp):
                for s in signals_b["sp"]:
                    s.prime(sp)
                def load_conv(r, side):
                    if side < 2:
                        sp.wait_ge(gelu_ok.sem, gelu_ok.at(r, side - 2))
                    else:
                        sp.wait_ge(gelu_ok.sem, gelu_ok.at(r, 0))
                    rows = xc_d[bass.ds(tile_row(r, GROUP * side) + TILES, GROUP)].rearrange("t p n -> p t n")
                    sp.dma_start(xcg[:, side % 2].rearrange("p t r n -> p t (r n)"), rows).then_inc(xc_in[side % 2].sem, 16)

                def load_h2(r, n):
                    sp.wait_ge(xs_ok.sem, xs_ok.at(r, n - 4))
                    sp.wait_ge(hT_ps.sem, hT_ps.at(r, n - 4))
                    sp.dma_start(h2[:, n % 4, :], h2_d[bass.ds(tile_row(r, n) + TILES, 1)].rearrange("o p n -> (o p) n")) \
                        .then_inc(h2_in[n % 4].sem, 16)

                def load_x1(r, n):
                    sp.wait_ge(out_ok.sem, out_ok.at(r, n - 4))
                    sp.dma_start(x1[:, n % 4, :], x1_d[bass.ds(tile_row(r, n) + TILES, 1)].rearrange("o p n -> (o p) n")) \
                        .then_inc(x1_in[n % 4].sem, 16)

                def store(r, n):
                    sp.wait_ge(out_ok.sem, out_ok.at(r, n))
                    sp.dma_start(out[bass.ds(tile_row(r, n), 1)].rearrange("o p n -> (o p) n"), zn[:, n % 2, :]) \
                        .then_inc(out_st[n % 2].sem, 16)

                load_conv(0, 0)
                for dst, src in ((lstage[:], linw), (lb_raw[:], linb), (nid[:], negid)):
                    sp.dma_start(dst, src).then_inc(setup_b["lin"], 16)
                sp.dma_start(wstage[:], ffw.rearrange("(c p) n -> p c n", p=P)).then_inc(setup_b["ffw"], 16)
                sp.dma_start(ffb_b[:], ffb).then_inc(setup_b["ffw"], 16)
                load_h2(0, 0)
                sp.wait_ge(setup_b["pool"], 6)
                with sp.Fori(0, R) as r:
                    for n in range(SIDE):
                        if n == 0:
                            load_conv(r, 1)
                        if n == GROUP:
                            load_conv(r, 2)
                        load_h2(r, n + 1)
                        load_x1(r, n - 2)
                        store(r, n - LAG_OUT)
                for n in range(LAG_OUT):
                    if n < 2:
                        load_x1(R, n - 2)
                    store(R, n - LAG_OUT)
                sp.wait_ge(h2_in[0].sem, h2_in[0].at(R, 0))
                for s in out_st:
                    sp.wait_ge(s.sem, s.at(R, -1))

            @block.tensor
            def _(pe):
                for s in signals_b["pe"]:
                    s.prime(pe)
                pe.wait_ge(setup_b["lin"], 16 * 3)
                pe.wait_ge(setup_b["dve"], 3)

                def three(outp, n, total, stat, mov, fresh=True):
                    for k, (a, c) in enumerate(((0, 0), (0, 1), (1, 0))):
                        mm = nc.tensor.matmul(outp, stat(a), mov(c), start=(fresh and n == 0 and k == 0),
                                              stop=(n == total - 1 and k == 2))
                    return mm

                def logits(r, n):
                    group, j = (n // GROUP) % 2, n % GROUP
                    pe.wait_ge(xa_lo.sem, xa_lo.at(r, n // GROUP))
                    for s in range(2):
                        pe.wait_ge(ex_ok.sem, ex_ok.at(r, 2 * n - 2 + s))
                        nc.tensor.matmul(L_BANK[s], ones[:], lb[:, s, :], start=True, stop=False)
                        three(L_BANK[s], 0, 1, lambda a: xaT[:, group, a, j, s, :], lambda a: lw[:, s, a, :],
                              fresh=False).then_inc(lg_ps.sem, 1)

                def transposed(src, bank, signal):
                    for c in range(C):
                        mm = nc.tensor.matmul(bank[:, P * c:P * (c + 1)], src[:, P * c:P * (c + 1)], idn[:],
                                              is_transpose=True, start=(c == 0), stop=(c == C - 1), skip_group_check=True)
                    mm.then_inc(signal.sem, 1)

                def less_hi(bank, hi, signal):
                    nc.tensor.matmul(bank, nid[:], hi.rearrange("p c n -> p (c n)"), start=False, stop=True,
                                     skip_group_check=True).then_inc(signal.sem, 1)

                def product(bank, pair, signal):
                    for c in range(C):
                        mm = three(bank, c, C, lambda a: pair[:, a, c, :], lambda a: fw[:, a, c, :])
                    mm.then_inc(signal.sem, 1)

                def step(r, n, tail=False):
                    def due(lag):
                        return not tail or n - lag < 0
                    if not tail:
                        logits(r, n + 1)
                        pe.wait_ge(h2_in[n % 4].sem, h2_in[n % 4].at(r, n // 4))
                        pe.wait_ge(hT_lo.sem, hT_lo.at(r, n - 1))
                        transposed(h2[:, n % 4, :], HT_BANK, hT_ps)
                    m = n - 1
                    if due(1):
                        pe.wait_ge(hT_lo.sem, hT_lo.at(r, m))
                        pe.wait_ge(tf_ok.sem, tf_ok.at(r, m - 2))
                        product(F_BANK[m % 2], h2T[:, m % 2], full_ps)
                    if not tail:
                        pe.wait_ge(hT_hi.sem, hT_hi.at(r, n))
                        less_hi(HT_BANK, h2T[:, n % 2, 0], hm_ps)
                    if due(1):
                        pe.wait_ge(xs_ok.sem, xs_ok.at(r, m))
                        pe.wait_ge(xT_lo.sem, xT_lo.at(r, m - 1))
                        transposed(xs[:, m % 2, :], XT_BANK, xT_ps)
                    if due(LAG_IN):
                        k = n - LAG_IN
                        pe.wait_ge(xT_lo.sem, xT_lo.at(r, k))
                        pe.wait_ge(tin_ok.sem, tin_ok.at(r, k - 2))
                        product(I_BANK[k % 2], xsT[:, k % 2], in_ps)
                    if due(1):
                        pe.wait_ge(xT_hi.sem, xT_hi.at(r, m))
                        less_hi(XT_BANK, xsT[:, m % 2, 0], xm_ps)

                logits(0, 0)
                pe.wait_ge(setup_b["dve"], 5)
                pe.wait_ge(setup_b["pool"], 6)
                with pe.Fori(0, R) as r:
                    for n in range(SIDE):
                        step(r, n)
                for n in range(LAG_OUT):
                    step(R, n, tail=True)

            @block.scalar
            def _(act):
                for s in signals_b["act"]:
                    s.prime(act)
                def gelu(r, side):
                    slot = side % 2
                    act.wait_ge(xc_in[slot].sem, xc_in[slot].at(r, side // 2))
                    act.wait_ge(xa_lo.sem, xa_lo.at(r, side - 1))
                    for s in range(2):
                        i = nc.scalar.activation(xa[:, :, s, :], xcg[:, slot, :, s, :], ACT.Gelu, bias=bn_bi[:, s:s + 1],
                                                 scale=bn_sc[:, s:s + 1])
                    i.then_inc(gelu_ok.sem, 1)
                    act.wait_ge(gelu_ok.sem, gelu_ok.at(r, side))
                    act.wait_ge(lg_ps.sem, lg_ps.at(r, 2 * (GROUP * (side - 1)) - 1))
                    nc.scalar.activation(xaT[:, slot, 0].rearrange("p t s n -> p (t s n)"),
                                         xa[:].rearrange("p t s n -> p (t s n)"), ACT.Copy, scale=A_SCALE).then_inc(xa_hi.sem, 1)

                def exponentials(r, n):
                    for s in range(2):
                        i = 2 * n + s
                        act.wait_ge(mx_ok.sem, mx_ok.at(r, i))
                        nc.scalar.activation(nmx[:, s:s + 1], m8[:, s, 0:1], ACT.Copy, scale=-L_DOWN).then_inc(nmx_ok.sem, 1)
                    for s in range(2):
                        i = 2 * n + s
                        act.wait_ge(nmx_ok.sem, nmx_ok.at(r, i))
                        nc.scalar.activation(e8[:, s, :], m8[:, s, :], ACT.Exp, bias=nmx[:, s:s + 1], scale=L_DOWN) \
                            .then_inc(e8_ok.sem, 1)
                        act.wait_ge(sel_ok.sem, sel_ok.at(r, i - 8))
                        nc.scalar.activation(ex[:, n % 4, s, :], L_BANK[s], ACT.Exp, bias=nmx[:, s:s + 1], scale=L_DOWN,
                                             accum_out=den[:, n % 2, s:s + 1]).then_inc(ex_ok.sem, 1)

                def half(r, k, before, bank, dst, after):
                    act.wait_ge(before.sem, before.at(r, k))
                    nc.scalar.activation(dst, bank.rearrange("p (c n) -> p c n", c=C), ACT.Copy, scale=W_SCALE) \
                        .then_inc(after.sem, 1)

                def step(r, n, tail=False):
                    def due(lag):
                        return not tail or n - lag < 0
                    if not tail:
                        half(r, n, hT_ps, HT_BANK, h2T[:, n % 2, 0], hT_hi)
                    if due(1):
                        k = n - 1
                        act.wait_ge(full_ps.sem, full_ps.at(r, k))
                        act.wait_ge(rden_ok.sem, rden_ok.at(r, k))
                        act.wait_ge(zn_ok.sem, zn_ok.at(r, k - 8))
                        nc.scalar.activation(zz[:, k % 8, :], F_BANK[k % 2], ACT.Copy, scale=rden[:, k % 4, OUT:OUT + 1]) \
                            .then_inc(tf_ok.sem, 1)
                    if not tail:
                        half(r, n, hm_ps, HT_BANK, h2T[:, n % 2, 1], hT_lo)
                    if due(1):
                        half(r, n - 1, xT_ps, XT_BANK, xsT[:, (n - 1) % 2, 0], xT_hi)
                    if not tail:
                        exponentials(r, n + 1)
                    if due(LAG_IN):
                        k = n - LAG_IN
                        act.wait_ge(in_ps.sem, in_ps.at(r, k))
                        act.wait_ge(z0_ok.sem, z0_ok.at(r, k - 2))
                        nc.scalar.activation(t_in[:, k % 2, :], I_BANK[k % 2], ACT.Copy, scale=rden[:, k % 4, IN:IN + 1]) \
                            .then_inc(tin_ok.sem, 1)
                    if due(1):
                        half(r, n - 1, xm_ps, XT_BANK, xsT[:, (n - 1) % 2, 1], xT_lo)
                    if due(LAG_STAT):
                        k = n - LAG_STAT
                        z = zz[:, k % 8, :]
                        act.wait_ge(z_ok.sem, z_ok.at(r, k))
                        act.wait_ge(zsq_ok.sem, zsq_ok.at(r, k - 1))
                        nc.scalar.activation(junk[:], z, ACT.Copy, accum_out=zsum[:, k % 2:k % 2 + 1]).then_inc(zsum_ok.sem, 1)
                        act.wait_ge(zsum_ok.sem, zsum_ok.at(r, k))
                        nc.scalar.activation(zneg[:, k % 4:k % 4 + 1], zsum[:, k % 2:k % 2 + 1], ACT.Copy, scale=-1.0 / D) \
                            .then_inc(zneg_ok.sem, 1)
                        act.wait_ge(zneg_ok.sem, zneg_ok.at(r, k))
                        nc.scalar.activation(junk[:], z, ACT.Square, bias=zneg[:, k % 4:k % 4 + 1],
                                             accum_out=zsq[:, k % 2:k % 2 + 1]).then_inc(zsq_ok.sem, 1)
                    if due(LAG_NORM):
                        k = n - LAG_NORM
                        act.wait_ge(zsc_ok.sem, zsc_ok.at(r, k))
                        act.wait_ge(out_st[k % 2].sem, out_st[k % 2].at(r, k // 2 - 1))
                        nc.scalar.activation(zn[:, k % 2, :], zz[:, k % 8, :], ACT.Identity, bias=zsc[:, k % 2, 1:2],
                                             scale=zsc[:, k % 2, 0:1]).then_inc(zn_ok.sem, 1)
                    if not tail and n == 1:
                        gelu(r, 1)
                    if not tail and n == GROUP + 1:
                        gelu(r, 2)

                act.wait_ge(setup_b["lin"], 16 * 3)
                nc.scalar.activation(lw[:, :, 0, :], lstage[:], ACT.Copy, scale=W_SCALE).then_inc(setup_b["act"], 1)
                nc.scalar.activation(lb_raw[:], lb_raw[:], ACT.Copy, scale=W_SCALE).then_inc(setup_b["act"], 1)
                act.wait_ge(setup_b["act"], 2)
                nc.scalar.activation(lb_hi[:], lb_raw[:], ACT.Copy).then_inc(setup_b["act"], 1)
                act.wait_ge(setup_b["pool"], 5)
                gelu(0, 0)
                act.wait_ge(setup_b["ffw"], 16 * 2)
                nc.scalar.activation(fw[:, 0], wstage[:], ACT.Copy, scale=W_SCALE).then_inc(setup_b["act"], 1)
                exponentials(0, 0)
                act.wait_ge(setup_b["pool"], 6)
                act.wait_ge(setup_b["dve"], 5)
                with act.Fori(0, R) as r:
                    for n in range(SIDE):
                        step(r, n)
                for n in range(LAG_OUT):
                    step(R, n, tail=True)

            @block.vector
            def _(dve):
                for s in signals_b["dve"]:
                    s.prime(dve)
                for s in range(2):
                    i = nc.vector.bn_aggr(bn_mv[:, s, :], bn_all[:, TILES:, s, :])
                i.then_inc(setup_b["dve"], 1)
                for a in (ex[:, 3], rest[:, 1], h2T[:, 1], xsT[:, 0], zn[:, 0]):
                    nc.vector.memset(a, 0.0)
                nc.vector.memset(ones[:], -A_SCALE)
                dve.wait_ge(setup_b["act"], 1)
                nc.vector.scalar_tensor_tensor(lw[:, :, 1, :], lstage[:], W_SCALE, lw[:, :, 0, :], ALU.mult, ALU.subtract) \
                    .then_inc(setup_b["dve"], 1)
                dve.wait_ge(setup_b["act"], 3)
                nc.vector.scalar_tensor_tensor(lb[:], lb_hi[:], idn[0:2, 1:2], lb_raw[:], ALU.mult, ALU.subtract) \
                    .then_inc(setup_b["dve"], 1)

                def gelu_lo(r, side):
                    dve.wait_ge(xa_hi.sem, xa_hi.at(r, side))
                    hi, lo = (xaT[:, side % 2, a].rearrange("p t s n -> p (t s n)") for a in range(2))
                    nc.vector.scalar_tensor_tensor(lo, xa[:].rearrange("p t s n -> p (t s n)"), A_SCALE, hi, ALU.mult,
                                                   ALU.subtract).then_inc(xa_lo.sem, 1)

                def largest(r, n):
                    for s in range(2):
                        wait_apart(dve, lg_ps, lg_ps.at(r, 2 * n + s))
                        nc.vector.max(m8[:, s, :], L_BANK[s]).then_inc(mx_ok.sem, 1)

                def step(r, n):
                    first = TOP_STEPS * n

                    def remove(k, s, dst, eight, src):
                        if k == 0:
                            dve.wait_ge(ex_ok.sem, ex_ok.at(r, 2 * n + s))
                        if k == 6:
                            dve.wait_ge(sel_ok.sem, sel_ok.at(r, 2 * (n - 2) + 1))
                        wait_apart(dve, top_ok, top_ok.at(r, first + 2 * k + s - 2))
                        nc.vector.match_replace(dst, eight, src, 0.0).then_inc(top_ok.sem, 1)

                    def next_eight(k, s, dst, src):
                        wait_apart(dve, top_ok, top_ok.at(r, first + 2 * k + s - 2))
                        nc.vector.max(dst, src).then_inc(top_ok.sem, 1)

                    for s in range(2):
                        remove(0, s, cut[:, s, 0, :], e8[:, s, :], ex[:, n % 4, s, :])
                    for s in range(2):
                        next_eight(1, s, c8[:, s, 0, :], cut[:, s, 0, :])
                    for s in range(2):
                        remove(2, s, cut[:, s, 1, :], c8[:, s, 0, :], cut[:, s, 0, :])
                    dve.wait_ge(ex_ok.sem, ex_ok.at(r, 2 * n + 1))
                    nc.vector.reciprocal(rden[:, n % 4, :], den[:, n % 2, :]).then_inc(rden_ok.sem, 1)
                    largest(r, n + 1)
                    for s in range(2):
                        next_eight(3, s, c8[:, s, 1, :], cut[:, s, 1, :])
                    for s in range(2):
                        remove(4, s, cut[:, s, 0, :], c8[:, s, 1, :], cut[:, s, 1, :])
                    if n == 2:
                        gelu_lo(r, 1)
                    if n == GROUP + 2:
                        gelu_lo(r, 2)
                    for s in range(2):
                        next_eight(5, s, c8[:, s, 2, :], cut[:, s, 0, :])
                    for s in range(2):
                        remove(6, s, rest[:, n % 2, s, :], c8[:, s, 2, :], cut[:, s, 0, :])

                gelu_lo(0, 0)
                dve.wait_ge(setup_b["ffw"], 16 * 2)
                nc.vector.tensor_scalar(ffb_b[:], ffb_b[:], FF_SCALE, None, ALU.mult).then_inc(setup_b["dve"], 1)
                largest(0, 0)
                dve.wait_ge(setup_b["act"], 4)
                nc.vector.scalar_tensor_tensor(fw[:, 1], wstage[:], W_SCALE, fw[:, 0], ALU.mult, ALU.subtract) \
                    .then_inc(setup_b["dve"], 1)
                dve.wait_ge(setup_b["pool"], 6)
                with dve.Fori(0, R) as r:
                    for n in range(SIDE):
                        step(r, n)

            @block.gpsimd
            def _(pool):
                for s in signals_b["pool"]:
                    s.prime(pool)
                pool.wait_ge(setup_b["dve"], 1)
                for n, op in enumerate((
                        lambda: nc.gpsimd.tensor_scalar(bn_ve[:], bn_mv[:, :, 1], EPS, None, ALU.add),
                        lambda: nc.gpsimd.tensor_tensor(bn_ve[:], bn_ve[:], expo[:, 0:2], ALU.pow),
                        lambda: nc.gpsimd.tensor_tensor(bn_sc[:], bn_ve[:], chan_s[:, :, 1], ALU.mult),
                        lambda: nc.gpsimd.tensor_tensor(bn_bi[:], bn_mv[:, :, 0], bn_sc[:], ALU.mult),
                        lambda: nc.gpsimd.tensor_tensor(bn_bi[:], chan_s[:, :, 2], bn_bi[:], ALU.subtract))):
                    if n:
                        pool.wait_ge(setup_b["pool"], n)
                    op().then_inc(setup_b["pool"], 1)
                for a in (h2[:, 3], x1[:], zz[:, 3:7], t_in[:, 1], rden[:], zneg[:], zsc[:]):
                    nc.gpsimd.memset(a, 0.0)
                nc.gpsimd.memset(zsq[:], 0.0).then_inc(setup_b["pool"], 1)
                pool.wait_ge(setup_b["dve"], 4)

                def step(r, n, tail=False):
                    def due(lag):
                        return not tail or n - lag < 0
                    if due(1):
                        k = n - 1
                        top = TOP_STEPS * (k + 1) - 1
                        slot = k % 2
                        pool.wait_ge(top_ok.sem, top_ok.at(r, top))
                        pool.wait_ge(xs_ok.sem, xs_ok.at(r, k - 2))
                        nc.gpsimd.tensor_tensor(sel[:, slot, IN, :], ex[:, k % 4, IN, :], rest[:, slot, IN, :], ALU.subtract) \
                            .then_inc(sel_ok.sem, 1)
                        pool.wait_ge(sel_ok.sem, sel_ok.at(r, 2 * k))
                        pool.wait_ge(xT_ps.sem, xT_ps.at(r, k - 2))
                        pool.wait_ge(h2_in[k % 4].sem, h2_in[k % 4].at(r, k // 4))
                        nc.gpsimd.tensor_tensor(xs[:, slot, :], sel[:, slot, IN, :], h2[:, k % 4, :], ALU.mult).then_inc(xs_ok.sem, 1)
                        pool.wait_ge(t1_ok.sem, t1_ok.at(r, k - 2))
                        nc.gpsimd.tensor_tensor(sel[:, slot, OUT, :], ex[:, k % 4, OUT, :], rest[:, slot, OUT, :], ALU.subtract) \
                            .then_inc(sel_ok.sem, 1)
                        pool.wait_ge(sel_ok.sem, sel_ok.at(r, 2 * k + 1))
                        pool.wait_ge(tf_ok.sem, tf_ok.at(r, k))
                        nc.gpsimd.tensor_tensor(zz[:, k % 8, :], zz[:, k % 8, :], sel[:, slot, OUT, :], ALU.mult).then_inc(t1_ok.sem, 1)
                    if due(LAG_Z):
                        k = n - LAG_Z
                        z = zz[:, k % 8, :]
                        pool.wait_ge(tin_ok.sem, tin_ok.at(r, k))
                        pool.wait_ge(t1_ok.sem, t1_ok.at(r, k))
                        nc.gpsimd.tensor_tensor(z, z, t_in[:, k % 2, :], ALU.add).then_inc(z0_ok.sem, 1)
                        pool.wait_ge(z0_ok.sem, z0_ok.at(r, k))
                        nc.gpsimd.tensor_tensor(z, z, ffb_b[:], ALU.add).then_inc(z_ok.sem, 1)
                    if due(LAG_NORM):
                        k = n - LAG_NORM
                        wait_apart(pool, zsq_ok, zsq_ok.at(r, k))
                        nc.gpsimd.tensor_scalar(zvar[:], zsq[:, k % 2:k % 2 + 1], 1.0 / D, EPS * FF_SCALE * FF_SCALE, ALU.mult,
                                                ALU.add).then_inc(zvar_ok.sem, 1)
                        pool.wait_ge(zvar_ok.sem, zvar_ok.at(r, k))
                        nc.gpsimd.tensor_tensor(zsc[:, k % 2, 0:1], zvar[:], expo[:, 0:1], ALU.pow).then_inc(zrs_ok.sem, 1)
                        pool.wait_ge(zrs_ok.sem, zrs_ok.at(r, k))
                        nc.gpsimd.tensor_tensor(zsc[:, k % 2, 1:2], zneg[:, k % 4:k % 4 + 1], zsc[:, k % 2, 0:1], ALU.mult) \
                            .then_inc(zsc_ok.sem, 1)
                    if due(LAG_OUT):
                        k = n - LAG_OUT
                        pool.wait_ge(zn_ok.sem, zn_ok.at(r, k))
                        pool.wait_ge(x1_in[k % 4].sem, x1_in[k % 4].at(r, k // 4))
                        nc.gpsimd.tensor_tensor(zn[:, k % 2, :], zn[:, k % 2, :], x1[:, k % 4, :], ALU.add).then_inc(out_ok.sem, 1)

                with pool.Fori(0, R) as r:
                    for n in range(SIDE):
                        step(r, n)
                for n in range(LAG_OUT):
                    step(R, n, tail=True)


OUT_ROWS = B * TILES + 8


def kernel(**inputs):
    import concourse.bacc as bacc
    from concourse.bass_utils import run_bass_kernel_spmd

    def a(name):
        return np.asarray(inputs["L0_" + name])

    def rows(v):
        return np.ascontiguousarray(np.broadcast_to(v.reshape(1, -1), (P, v.size)))

    def columns(v):
        return v.reshape(-1, P).T

    ident = np.eye(P, dtype=np.float32)
    negid = (-np.eye(P) / W_SCALE).astype(np.float16)
    mask = np.zeros((P, 512), np.float32)
    mask[:, 384:] = np.where(np.arange(P)[None, :] > np.arange(P)[:, None], -NEG / S_SCALE, 0.0)
    arrays = {
        "x": a("attn_x"),
        "wqkvo": np.stack([a("attn_W" + w) for w in "qkvo"]),
        "bqk": np.ascontiguousarray(np.stack([columns(a("attn_b" + w)) for w in "qk"], 1)),
        "bv": rows(a("attn_bv")), "bo": rows(a("attn_bo")),
        "ffw": a("ffn_weight"), "ffb": rows(a("ffn_bias")),
        "linw": np.ascontiguousarray(np.stack([a("ffn_so_lin_w").T, a("ffn_si_lin_w").T], 1)),
        "linb": np.stack([np.stack([a("ffn_so_lin_b"), a("ffn_si_lin_b")])] * 2),
        "convw": np.ascontiguousarray(np.stack([rows(a("ffn_so_conv_w").ravel()), rows(a("ffn_si_conv_w").ravel())], 1)),
        "chan": np.ascontiguousarray(np.stack([np.stack([a(f"ffn_{s}_{n}") for n in ("conv_b", "gamma", "beta")], 1)
                                               for s in ("so", "si")], 1)),
        "ident": ident, "negid": negid, "mask": mask,
    }
    nc = bacc.Bacc("TRN2", target_bir_lowering=False, num_devices=1)
    aps = [nc.dram_tensor(n, v.shape, mybir.dt.from_np(v.dtype), kind="ExternalInput").ap() for n, v in arrays.items()]
    out = nc.dram_tensor("out", [OUT_ROWS, P, D], F32, kind="ExternalOutput").ap()
    layer_block(nc, *aps, out)
    r = run_bass_kernel_spmd(nc, [arrays], core_ids=[0])
    return np.asarray(r.results[0]["out"])[:B * TILES].reshape(B, S, D)
```
